# Optimizing a Trainium2 kernel written in Bass

```python
import numpy as np
import jax
import jax.numpy as jnp

def _softmax(x, axis=-1):
    return jax.nn.softmax(x, axis=axis)

def _gelu(x):
    return jax.nn.gelu(x, approximate=True)

def _silu(x):
    return jax.nn.silu(x)

def _sigmoid(x):
    return jax.nn.sigmoid(x)

def _layernorm(x, axis=-1, eps=1e-05):
    m = jnp.mean(x, axis=axis, keepdims=True)
    v = jnp.var(x, axis=axis, keepdims=True)
    return (x - m) / jnp.sqrt(v + eps)

def _scatter_add(tgt, idx, src, axis=0):
    return tgt.at[idx].add(src)

def _segment_sum(src, seg, n):
    return jax.ops.segment_sum(src, seg, n)
kernel_name = 'mk_seq_postln_d2_jaxref_r8_5f9317'

def setup_inputs(seed: int=0):
    np.random.seed(seed)
    _w = jnp.asarray

    def _L0_attn_setup():
        import jax, jax.numpy as jnp
        import numpy as np
        EMBED = 128
        HEADS = 16
        key = jax.random.key(seed)
        ks = jax.random.split(key, 6)
        N, S = (1, 512)
        half = EMBED // 2
        x = jax.random.normal(ks[0], (N, S, EMBED), dtype=jnp.float32)
        Wq = jax.random.normal(ks[1], (half, half), dtype=jnp.float32) * 0.02
        Wk = jax.random.normal(ks[2], (half, half), dtype=jnp.float32) * 0.02
        Wv = jax.random.normal(ks[3], (half, half), dtype=jnp.float32) * 0.02
        Wo = jax.random.normal(ks[4], (EMBED, half), dtype=jnp.float32) * 0.02
        bo = jnp.zeros((EMBED,), dtype=jnp.float32)
        return {'x': x, 'Wq': Wq, 'Wk': Wk, 'Wv': Wv, 'Wo': Wo, 'bo': bo}
    _L0_attn_in = _L0_attn_setup()

    def _L0_ffn_setup():
        import jax, jax.numpy as jnp
        import numpy as np
        D_MODEL = 128
        N_HEADS = 16
        HEAD_DIM = D_MODEL // N_HEADS
        FFN_DIM = 512
        N_EXPERTS = 8
        TOP_K = 2
        BATCH = 4
        SEQ = 128

        def _layernorm(x, w, b, eps=1e-05):
            mu = jnp.mean(x, axis=-1, keepdims=True)
            var = jnp.mean(jnp.square(x - mu), axis=-1, keepdims=True)
            return (x - mu) * jax.lax.rsqrt(var + eps) * w + b

        def _causal_attention(nx, Wqkv, bqkv, Wo, bo):
            B, S, D = nx.shape
            qkv = nx @ Wqkv + bqkv
            q, k, v = jnp.split(qkv, 3, axis=-1)
            q = q.reshape(B, S, N_HEADS, HEAD_DIM)
            k = k.reshape(B, S, N_HEADS, HEAD_DIM)
            v = v.reshape(B, S, N_HEADS, HEAD_DIM)
            scores = jnp.einsum('bqhd,bkhd->bhqk', q, k) / jnp.sqrt(jnp.float32(HEAD_DIM))
            causal = jnp.tril(jnp.ones((S, S), bool))
            scores = jnp.where(causal, scores, jnp.finfo(scores.dtype).min)
            attn = jax.nn.softmax(scores, axis=-1)
            out = jnp.einsum('bhqk,bkhd->bqhd', attn, v).reshape(B, S, D)
            return out @ Wo + bo

        def _moe_ffn(nx, gate_W, fc1_w, fc1_b, fc2_w, fc2_b):
            gate_logits = nx @ gate_W
            topk_vals, topk_idx = jax.lax.top_k(gate_logits, TOP_K)
            gate_w = jax.nn.softmax(topk_vals, axis=-1)
            dense_gates = jnp.sum(jax.nn.one_hot(topk_idx, N_EXPERTS, dtype=nx.dtype) * gate_w[..., None], axis=-2)
            moe_out = jnp.zeros_like(nx)
            for e in range(N_EXPERTS):
                h = jax.nn.gelu(jnp.einsum('bsd,fd->bsf', nx, fc1_w[e]) + fc1_b[e], approximate=False)
                y = jnp.einsum('bsf,df->bsd', h, fc2_w[e]) + fc2_b[e]
                moe_out = moe_out + y * dense_gates[..., e:e + 1]
            return moe_out
        key = jax.random.key(seed)
        ks = jax.random.split(key, 12)
        s = lambda k, shape, scale: jax.random.normal(k, shape, dtype=jnp.float32) * scale
        inp = {'x': s(ks[0], (BATCH, SEQ, D_MODEL), 1.0), 'ln1_w': jnp.ones((D_MODEL,), jnp.float32), 'ln1_b': jnp.zeros((D_MODEL,), jnp.float32), 'ln2_w': jnp.ones((D_MODEL,), jnp.float32), 'ln2_b': jnp.zeros((D_MODEL,), jnp.float32), 'Wqkv': s(ks[1], (D_MODEL, 3 * D_MODEL), 0.02), 'bqkv': jnp.zeros((3 * D_MODEL,), jnp.float32), 'Wo': s(ks[2], (D_MODEL, D_MODEL), 0.02), 'bo': jnp.zeros((D_MODEL,), jnp.float32), 'gate_W': s(ks[3], (D_MODEL, N_EXPERTS), 0.02), 'fc1_w': s(ks[4], (N_EXPERTS, FFN_DIM, D_MODEL), (2.0 / D_MODEL) ** 0.5), 'fc1_b': jnp.zeros((N_EXPERTS, FFN_DIM), jnp.float32), 'fc2_w': s(ks[5], (N_EXPERTS, D_MODEL, FFN_DIM), (1.0 / FFN_DIM) ** 0.5), 'fc2_b': jnp.zeros((N_EXPERTS, D_MODEL), jnp.float32)}
        return inp
    _L0_ffn_in = _L0_ffn_setup()

    def _L1_attn_setup():
        import jax, jax.numpy as jnp
        import numpy as np
        from math import sqrt
        NUM_HEADS = 16
        key = jax.random.key(seed)
        ks = jax.random.split(key, 5)
        B, S, H = (2, 256, 128)
        scale = 0.02
        return {'x': jax.random.normal(ks[0], (B, S, H), dtype=jnp.float32), 'W_qkv': jax.random.normal(ks[1], (3 * H, H), dtype=jnp.float32) * scale, 'b_qkv': jax.random.normal(ks[2], (3 * H,), dtype=jnp.float32) * scale, 'W_o': jax.random.normal(ks[3], (H, H), dtype=jnp.float32) * scale, 'b_o': jax.random.normal(ks[4], (H,), dtype=jnp.float32) * scale}
    _L1_attn_in = _L1_attn_setup()

    def _L1_ffn_setup():
        import jax, jax.numpy as jnp
        import numpy as np
        B, S, H = (1, 256, 128)
        E = 16
        I = 96
        TOPK = 4
        G = 4
        TOPK_G = 2
        SCALE = 2.5
        N_SHARED = 1

        def _route(x, gate_w, gate_bias):
            n = x.shape[0]
            logits = jnp.einsum('nh,eh->ne', x.astype(jnp.float32), gate_w)
            scores = jax.nn.sigmoid(logits)
            sb = scores + gate_bias
            gs = sb.reshape(n, G, E // G)
            group_scores = jnp.sum(jax.lax.top_k(gs, 2)[0], axis=-1)
            _, gidx = jax.lax.top_k(group_scores, TOPK_G)
            gmask = jnp.sum(jax.nn.one_hot(gidx, G, dtype=sb.dtype), axis=1)
            emask = jnp.repeat(gmask, E // G, axis=-1)
            masked = jnp.where(emask > 0, sb, -jnp.inf)
            _, tidx = jax.lax.top_k(masked, TOPK)
            w = jnp.take_along_axis(scores, tidx, axis=1)
            w = w / (jnp.sum(w, axis=-1, keepdims=True) + 1e-20)
            return (tidx, w * SCALE)
        key = jax.random.key(seed)
        ks = jax.random.split(key, 9)

        def rn(k, shape, scale=0.02):
            return jax.random.normal(k, shape, dtype=jnp.float32) * scale
        return dict(hidden_states=jax.random.normal(ks[0], (B, S, H), dtype=jnp.float32), gate_w=rn(ks[1], (E, H)), gate_bias=jax.random.normal(ks[2], (E,), dtype=jnp.float32) * 0.1, w1=rn(ks[3], (E, I, H)), w2=rn(ks[4], (E, H, I)), w3=rn(ks[5], (E, I, H)), ws1=rn(ks[6], (I * N_SHARED, H)), ws2=rn(ks[7], (H, I * N_SHARED)), ws3=rn(ks[8], (I * N_SHARED, H)))
    _L1_ffn_in = _L1_ffn_setup()
    _d = {'L0_attn_x': _L0_attn_in['x'], 'L0_attn_Wq': _L0_attn_in['Wq'], 'L0_attn_Wk': _L0_attn_in['Wk'], 'L0_attn_Wv': _L0_attn_in['Wv'], 'L0_attn_Wo': _L0_attn_in['Wo'], 'L0_attn_bo': _L0_attn_in['bo'], 'L0_ffn_ln1_w': _L0_ffn_in['ln1_w'], 'L0_ffn_ln1_b': _L0_ffn_in['ln1_b'], 'L0_ffn_ln2_w': _L0_ffn_in['ln2_w'], 'L0_ffn_ln2_b': _L0_ffn_in['ln2_b'], 'L0_ffn_Wqkv': _L0_ffn_in['Wqkv'], 'L0_ffn_bqkv': _L0_ffn_in['bqkv'], 'L0_ffn_Wo': _L0_ffn_in['Wo'], 'L0_ffn_bo': _L0_ffn_in['bo'], 'L0_ffn_gate_W': _L0_ffn_in['gate_W'], 'L0_ffn_fc1_w': _L0_ffn_in['fc1_w'], 'L0_ffn_fc1_b': _L0_ffn_in['fc1_b'], 'L0_ffn_fc2_w': _L0_ffn_in['fc2_w'], 'L0_ffn_fc2_b': _L0_ffn_in['fc2_b'], 'L1_attn_W_qkv': _L1_attn_in['W_qkv'], 'L1_attn_b_qkv': _L1_attn_in['b_qkv'], 'L1_attn_W_o': _L1_attn_in['W_o'], 'L1_attn_b_o': _L1_attn_in['b_o'], 'L1_ffn_gate_w': _L1_ffn_in['gate_w'], 'L1_ffn_gate_bias': _L1_ffn_in['gate_bias'], 'L1_ffn_w1': _L1_ffn_in['w1'], 'L1_ffn_w2': _L1_ffn_in['w2'], 'L1_ffn_w3': _L1_ffn_in['w3'], 'L1_ffn_ws1': _L1_ffn_in['ws1'], 'L1_ffn_ws2': _L1_ffn_in['ws2'], 'L1_ffn_ws3': _L1_ffn_in['ws3']}
    _x0 = _d['L0_attn_x']
    _d['L0_attn_x'] = jax.random.normal(jax.random.fold_in(jax.random.key(seed), 1), (16, 256, 128), dtype=_x0.dtype)
    del _x0
    return _d

def reference(L0_attn_x, L0_attn_Wq, L0_attn_Wk, L0_attn_Wv, L0_attn_Wo, L0_attn_bo, L0_ffn_ln1_w, L0_ffn_ln1_b, L0_ffn_ln2_w, L0_ffn_ln2_b, L0_ffn_Wqkv, L0_ffn_bqkv, L0_ffn_Wo, L0_ffn_bo, L0_ffn_gate_W, L0_ffn_fc1_w, L0_ffn_fc1_b, L0_ffn_fc2_w, L0_ffn_fc2_b, L1_attn_W_qkv, L1_attn_b_qkv, L1_attn_W_o, L1_attn_b_o, L1_ffn_gate_w, L1_ffn_gate_bias, L1_ffn_w1, L1_ffn_w2, L1_ffn_w3, L1_ffn_ws1, L1_ffn_ws2, L1_ffn_ws3):

    def _L0_attn_ref(x, Wq, Wk, Wv, Wo, bo):
        import jax, jax.numpy as jnp
        import numpy as np
        EMBED = 128
        HEADS = 16
        N, S, E = x.shape
        H = HEADS
        Dh = E // 2 // H
        scale = float(E // H) ** 0.5
        left = x[..., :E // 2]
        q = (left @ Wq.T).reshape(N, S, H, Dh)
        k = (left @ Wk.T).reshape(N, S, H, Dh)
        v = (left @ Wv.T).reshape(N, S, H, Dh)
        energy = jnp.einsum('nqhd,nkhd->nqkh', q, k)
        att = jax.nn.softmax(energy / scale, axis=2)
        out = jnp.einsum('nqkh,nkhd->nqhd', att, v)
        out = out.reshape(N, S, E // 2)
        return out @ Wo.T + bo

    def _L0_ffn_ref(x, ln1_w, ln1_b, ln2_w, ln2_b, Wqkv, bqkv, Wo, bo, gate_W, fc1_w, fc1_b, fc2_w, fc2_b):
        import jax, jax.numpy as jnp
        import numpy as np
        D_MODEL = 128
        N_HEADS = 16
        HEAD_DIM = D_MODEL // N_HEADS
        FFN_DIM = 512
        N_EXPERTS = 8
        TOP_K = 2
        BATCH = 4
        SEQ = 128

        def _layernorm(x, w, b, eps=1e-05):
            mu = jnp.mean(x, axis=-1, keepdims=True)
            var = jnp.mean(jnp.square(x - mu), axis=-1, keepdims=True)
            return (x - mu) * jax.lax.rsqrt(var + eps) * w + b

        def _causal_attention(nx, Wqkv, bqkv, Wo, bo):
            B, S, D = nx.shape
            qkv = nx @ Wqkv + bqkv
            q, k, v = jnp.split(qkv, 3, axis=-1)
            q = q.reshape(B, S, N_HEADS, HEAD_DIM)
            k = k.reshape(B, S, N_HEADS, HEAD_DIM)
            v = v.reshape(B, S, N_HEADS, HEAD_DIM)
            scores = jnp.einsum('bqhd,bkhd->bhqk', q, k) / jnp.sqrt(jnp.float32(HEAD_DIM))
            causal = jnp.tril(jnp.ones((S, S), bool))
            scores = jnp.where(causal, scores, jnp.finfo(scores.dtype).min)
            attn = jax.nn.softmax(scores, axis=-1)
            out = jnp.einsum('bhqk,bkhd->bqhd', attn, v).reshape(B, S, D)
            return out @ Wo + bo

        def _moe_ffn(nx, gate_W, fc1_w, fc1_b, fc2_w, fc2_b):
            gate_logits = nx @ gate_W
            topk_vals, topk_idx = jax.lax.top_k(gate_logits, TOP_K)
            gate_w = jax.nn.softmax(topk_vals, axis=-1)
            dense_gates = jnp.sum(jax.nn.one_hot(topk_idx, N_EXPERTS, dtype=nx.dtype) * gate_w[..., None], axis=-2)
            moe_out = jnp.zeros_like(nx)
            for e in range(N_EXPERTS):
                h = jax.nn.gelu(jnp.einsum('bsd,fd->bsf', nx, fc1_w[e]) + fc1_b[e], approximate=False)
                y = jnp.einsum('bsf,df->bsd', h, fc2_w[e]) + fc2_b[e]
                moe_out = moe_out + y * dense_gates[..., e:e + 1]
            return moe_out
        nx = _layernorm(x, ln1_w, ln1_b)
        attn_out = _causal_attention(nx, Wqkv, bqkv, Wo, bo)
        x = x + attn_out
        nx2 = _layernorm(x, ln2_w, ln2_b)
        moe_out = _moe_ffn(nx2, gate_W, fc1_w, fc1_b, fc2_w, fc2_b)
        return x + moe_out

    def _L1_attn_ref(x, W_qkv, b_qkv, W_o, b_o):
        import jax, jax.numpy as jnp
        import numpy as np
        from math import sqrt
        NUM_HEADS = 16
        B, S, H = x.shape
        nh = NUM_HEADS
        hd = H // nh
        qkv = x @ W_qkv.T + b_qkv
        Q, K, V = (qkv[..., :H], qkv[..., H:2 * H], qkv[..., 2 * H:])
        Q = Q.reshape(B, S, nh, hd)
        K = K.reshape(B, S, nh, hd)
        V = V.reshape(B, S, nh, hd)
        scores = jnp.einsum('bqhd,bkhd->bhqk', Q, K)
        causal = jnp.tril(jnp.ones((S, S), dtype=bool))
        scores = jnp.where(causal, scores, -jnp.inf)
        probs = jax.nn.softmax(scores / sqrt(hd), axis=-1)
        out = jnp.einsum('bkhd,bhqk->bqhd', V, probs)
        out = out.reshape(B, S, H)
        return out @ W_o.T + b_o

    def _L1_ffn_ref(hidden_states, gate_w, gate_bias, w1, w2, w3, ws1, ws2, ws3):
        import jax, jax.numpy as jnp
        import numpy as np
        B, S, H = (1, 256, 128)
        E = 16
        I = 96
        TOPK = 4
        G = 4
        TOPK_G = 2
        SCALE = 2.5
        N_SHARED = 1

        def _route(x, gate_w, gate_bias):
            n = x.shape[0]
            logits = jnp.einsum('nh,eh->ne', x.astype(jnp.float32), gate_w)
            scores = jax.nn.sigmoid(logits)
            sb = scores + gate_bias
            gs = sb.reshape(n, G, E // G)
            group_scores = jnp.sum(jax.lax.top_k(gs, 2)[0], axis=-1)
            _, gidx = jax.lax.top_k(group_scores, TOPK_G)
            gmask = jnp.sum(jax.nn.one_hot(gidx, G, dtype=sb.dtype), axis=1)
            emask = jnp.repeat(gmask, E // G, axis=-1)
            masked = jnp.where(emask > 0, sb, -jnp.inf)
            _, tidx = jax.lax.top_k(masked, TOPK)
            w = jnp.take_along_axis(scores, tidx, axis=1)
            w = w / (jnp.sum(w, axis=-1, keepdims=True) + 1e-20)
            return (tidx, w * SCALE)
        b, s, h = hidden_states.shape
        x = hidden_states.reshape(-1, h)
        tidx, tw = _route(x, gate_w, gate_bias)
        n = x.shape[0]
        combine = jnp.zeros((n, E), x.dtype).at[jnp.arange(n)[:, None], tidx].add(tw)
        g = jnp.einsum('nh,eih->nei', x, w1)
        u = jnp.einsum('nh,eih->nei', x, w3)
        hact = jax.nn.silu(g) * u * combine[:, :, None]
        y = jnp.einsum('nei,ehi->nh', hact, w2)
        shared = jnp.einsum('ni,hi->nh', jax.nn.silu(x @ ws1.T) * (x @ ws3.T), ws2)
        return (y + shared).reshape(b, s, h)
    x = L0_attn_x
    x = _layernorm(x + _L0_attn_ref(x, L0_attn_Wq, L0_attn_Wk, L0_attn_Wv, L0_attn_Wo, L0_attn_bo), axis=-1)
    x = _layernorm(x + _L0_ffn_ref(x, L0_ffn_ln1_w, L0_ffn_ln1_b, L0_ffn_ln2_w, L0_ffn_ln2_b, L0_ffn_Wqkv, L0_ffn_bqkv, L0_ffn_Wo, L0_ffn_bo, L0_ffn_gate_W, L0_ffn_fc1_w, L0_ffn_fc1_b, L0_ffn_fc2_w, L0_ffn_fc2_b), axis=-1)
    x = _layernorm(x + _L1_attn_ref(x, L1_attn_W_qkv, L1_attn_b_qkv, L1_attn_W_o, L1_attn_b_o), axis=-1)
    x = _layernorm(x + _L1_ffn_ref(x, L1_ffn_gate_w, L1_ffn_gate_bias, L1_ffn_w1, L1_ffn_w2, L1_ffn_w3, L1_ffn_ws1, L1_ffn_ws2, L1_ffn_ws3), axis=-1)
    return x

_drawn_inputs = setup_inputs


def setup_inputs(seed=0):
    import zlib

    import numpy as np

    out = dict(_drawn_inputs(seed))
    spreads = {'L0_attn_bo': (0.0, 0.1),
     'L0_ffn_ln1_w': (1.0, 0.6),
     'L0_ffn_ln1_b': (0.0, 0.371),
     'L0_ffn_ln2_w': (1.0, 0.2),
     'L0_ffn_ln2_b': (0.0, 0.1),
     'L0_ffn_bqkv': (0.0, 0.1),
     'L0_ffn_bo': (0.0, 0.1),
     'L0_ffn_fc1_b': (0.0, 0.347),
     'L0_ffn_fc2_b': (0.0, 0.1)}
    factors = {'L0_attn_Wq': 8.0,
     'L0_attn_Wk': 8.0,
     'L0_attn_Wv': 4.853,
     'L0_attn_Wo': 4.779,
     'L1_attn_W_qkv': 5.381,
     'L1_attn_b_qkv': 8.0,
     'L1_attn_W_o': 4.907,
     'L1_attn_b_o': 2.783,
     'L1_ffn_gate_w': 8.0,
     'L1_ffn_gate_bias': 8.0,
     'L1_ffn_w1': 8.0,
     'L1_ffn_w2': 8.0,
     'L1_ffn_w3': 8.0,
     'L1_ffn_ws1': 8.0,
     'L1_ffn_ws2': 8.0,
     'L1_ffn_ws3': 8.0}
    for name, (base, spread) in spreads.items():
        noise = np.random.default_rng([zlib.crc32(name.encode()), seed]).standard_normal(out[name].shape)
        drawn = base * np.exp(spread * noise) if base else spread * noise
        out[name] = jnp.asarray(drawn.astype(out[name].dtype))
    for name, factor in factors.items():
        out[name] = (out[name] * factor).astype(out[name].dtype)
    return out
```

```python
from contextlib import ExitStack

import numpy as np

import concourse.bass as bass
from concourse import mybir

F32 = mybir.dt.float32
F32R = mybir.dt.float32r
BF16 = mybir.dt.bfloat16
ALU = mybir.AluOpType
ACT = mybir.ActivationFunctionType
AX = mybir.AxisListType

P = 128
B, S, D = 16, 256, 128
H = 16
NT = S // P
ROWS = 32
NG = H * ROWS // P
GH = P // ROWS
EPS = 1e-5
MASKED = -1e30
SCALE = float(D // H) ** -0.5
RING = 3


class Turn:

    def __init__(self, i, c, total, ring):
        self.i, self.c, self.total, self.ring = i, c, total, ring
        self.r = c % ring

    def back(self, n):
        return Turn(self.i, self.c - n, self.total, self.ring)

    def there(self):
        return self.i is not None or 0 <= self.c < self.total

    def counted(self, per, more=0):
        fixed = self.c * per + more
        return min(fixed, self.total * per) if self.i is None else self.i * (self.ring * per) + fixed

    def used(self, per):
        fixed = (self.c // self.ring + 1) * per
        return fixed if self.i is None else self.i * per + fixed

    def of(self, view):
        if self.i is None:
            return view[self.c]
        return view[bass.ds(self.i * self.ring + self.c, 1)].rearrange("a p t d -> p (a t) d")


def positive(count):
    return not isinstance(count, int) or count > 0


def run_turns(eng, step, first, batches, turns, ring=RING):
    for t in range(first):
        step(Turn(None, t, batches, ring))
    rounds = (batches - first) // ring
    with eng.Fori(0, rounds) as i:
        for u in range(ring):
            step(Turn(i, first + u, batches, ring))
    for t in range(first + rounds * ring, turns):
        step(Turn(None, t, batches, ring))


def stage_semaphores(nc, ctx, tag):
    taken = []

    def sem(name):
        taken.append(nc.alloc_semaphore(f"{tag}_{name}"))
        return taken[-1]

    def clear():
        nc.clear_and_free_semaphores(taken)
        nc.all_engine_barrier()

    ctx.callback(clear)
    return sem


class Memory:

    def __init__(self, nc, ctx, tag, k_blocks):
        def sb(name, shape, dt=F32):
            return ctx.enter_context(nc.sbuf_tensor(f"{tag}_{name}", shape, dt))

        self.k_blocks = k_blocks
        self.k_stack = sb("k_stack", [P, NG, S], F32R)
        self.q_stack = sb("q_stack", [P, RING, NG, S], F32R)
        self.q_shift = sb("q_shift", [P, RING, NG, S], F32R)
        self.v_ones = sb("v_ones", [P, RING, NT, H, ROWS])
        self.probs = sb("probs", [P, 2 * GH, 2 * S])
        self.out_t = sb("out_t", [P, NG, S])
        self.neg_max = sb("neg_max", [P, NT, H])
        self.max_rows = sb("max_rows", [P, NT, H, ROWS])
        self.x_in = sb("x_in", [P, RING, NT, D])
        self.x_res = sb("x_res", [P, RING, NT, D])
        self.x_norm = sb("x_norm", [P, RING, NT, D])
        self.x_t = sb("x_t", [P, S])
        self.qk_hi = sb("qk_hi", [P, 2, S], F32R)
        self.qk_lo = sb("qk_lo", [P, 2, S], F32R)
        self.inv_sum = sb("inv_sum", [P, NT, H])
        self.out_n = sb("out_n", [P, NT, D])
        self.out_nt = sb("out_nt", [P, S])
        self.y = sb("y_sum", [P, NT, D])
        self.y_out = sb("y_out", [P, RING, NT, D])
        self.stats = sb("stats", [P, NT, 6])
        self.mean_var = sb("mean_var", [P, NT + 1, 2])
        self.var_eps = sb("var_eps", [P, NT])
        self.rstd = sb("rstd", [P, NT])
        self.stats_in = sb("stats_in", [P, NT, 6])
        self.mean_var_in = sb("mean_var_in", [P, NT + 1, 2])
        self.var_eps_in = sb("var_eps_in", [P, NT])
        self.rstd_in = sb("rstd_in", [P, NT])
        self.w_qk = sb("w_qk", [P, 2, P])
        self.w_v = sb("w_v", [P, D])
        self.w_o = sb("w_o", [P, D])
        self.sel = sb("sel", [P, 2, 2, NG, P], F32R)
        self.col = sb("col", [P, 8])
        self.rows_f32 = sb("rows_f32", [1, 2, D])
        self.wide = sb("wide", [P, 3, D])
        self.ident = sb("ident", [P, P])
        self.ident_bf = sb("ident_bf", [P, P], BF16)
        self.mask_f32 = sb("mask_f32", [P, 2, P])
        self.mask = sb("mask", [P, 2, GH, P], BF16)
        self.neg_half = sb("neg_half", [P, NT])



SLOTS = {
    "turn_max": 0, "turn_x": 2, "project_qk": 4, "turn_out": 7, "project_v": 8, "stack_k": 9, "turn_norm": 10, "stack_q": 12, "project_out": 14,
    "copy_x": 2, "copy_hi": 4, "copy_out_1": 5, "copy_v": 8, "copy_k": 9, "copy_norm": 10, "copy_q": 12, "copy_out_0": 13,
    "shift": 0, "split_lo": 5, "in_stats": 6, "divide": 7, "in_norm": 9, "add_out": 14, "norm_out": 15}
SLOTS_FULL = {**SLOTS, "turn_max": 1, "shift": 1, "turn_norm": 11, "copy_norm": 11}


def attention_stage(nc, tag, k_blocks, hd, causal, norm_in, norm_out, clear_blocks, x, y, w):
    row_hi, row_lo = 3 * hd, 3 * hd + 1
    HD = H * hd
    parts = 1 if hd == 4 else 2
    x_v = x.rearrange("b (t p) d -> b p t d", p=P)
    y_v = y.rearrange("b (t p) d -> b p t d", p=P)
    lag = 1 if norm_in else 0
    total = B + 3 + lag
    first = 7
    at = SLOTS if causal else SLOTS_FULL
    KM = 12 if causal else 16
    MAX_FROM = (H - KM) // 2
    if causal:
        max_ops = [(0, slice(0, GH), slice(0, P)), (1, slice(0, 2), slice(0, S)), (1, slice(2, 4), slice(0, S))]
    else:
        max_ops = [(qt, slice(2 * j, 2 * j + 2), slice(0, S)) for qt in range(NT) for j in range(2)]
    KM = NG * len(max_ops)
    CLEARED = 3 if clear_blocks else 2
    EW = S + P if causal else 2 * S

    with ExitStack() as ctx:
        m = Memory(nc, ctx, tag, k_blocks)

        sem = stage_semaphores(nc, ctx, tag)

        def psum(name, shape):
            return ctx.enter_context(nc.psum_tensor(f"{tag}_{name}", shape, F32))

        ps_max = psum("ps_max", [P, 2, 2 * S])
        ps_exp = psum("ps_exp", [P, 2, 2 * S])
        ps_out = psum("ps_out", [P, 2, S])
        ps_wide = psum("ps_wide", [P, NG, S])
        ps_small = psum("ps_small", [P, 2, S])

        sel_loaded = sem("sel_loaded")
        loaded_first = sem("loaded_first")
        loaded = sem("loaded")
        const_ready = sem("const_ready")
        cleared = sem("cleared")
        x_loaded = [sem(f"x_loaded{r}") for r in range(RING)]
        res_loaded = [sem(f"res_loaded{r}") for r in range(RING)]
        stored = [sem(f"stored{r}") for r in range(RING)]
        blocks_loaded = [sem(f"blocks_loaded{r}") for r in range(RING)]
        xt_done, qk_done, v_done = sem("xt_done"), sem("qk_done"), sem("v_done")
        k_stacked, q_stacked = sem("k_stacked"), sem("q_stacked")
        max_scored, max_turned = sem("max_scored"), sem("max_turned")
        exp_scored, weighed = sem("exp_scored"), sem("weighed")
        out_turned, norm_turned, projected = sem("out_turned"), sem("norm_turned"), sem("projected")
        xt_copied, hi_ready, v_copied = sem("xt_copied"), sem("hi_ready"), sem("v_copied")
        k_copied, q_copied = sem("k_copied"), sem("q_copied")
        exp_done, out_copied, norm_copied = sem("exp_done"), sem("out_copied"), sem("norm_copied")
        lo_ready, max_done, max_hi, rows_ready = sem("lo_ready"), sem("max_done"), sem("max_hi"), sem("rows_ready")
        shifted, inv_done, divided, summed = sem("shifted"), sem("inv_done"), sem("divided"), sem("summed")
        stats_done, aggr_done, eps_done, y_done = sem("stats_done"), sem("aggr_done"), sem("eps_done"), sem("y_done")
        v_cleared = sem("v_cleared")
        in_stats, in_aggr, in_eps, in_normed = sem("in_stats"), sem("in_aggr"), sem("in_eps"), sem("in_normed")
        bias_added, rstd_done = sem("bias_added"), sem("rstd_done")
        in_rstd, in_scaled, in_ready = sem("in_rstd"), sem("in_scaled"), sem("in_ready")

        later = [(m.w_v[:, 0:HD], w["v"]), (m.rows_f32[:], w["rows"]), (m.wide[:], w["wide"]), (m.mask_f32[:], w["masks"]), (m.w_o[0:HD, :], w["o"])]
        LOADED = 16 * len(later)

        block = ctx.enter_context(nc.Block())

        @block.sync
        def _(sp):
            for dst, src in ((m.ident[:], w["ident"]), (m.w_qk[:], w["qk"]), (m.col[:], w["col"])):
                sp.dma_start(dst, src).then_inc(loaded_first, 16)

            def step(t):
                if t.there():
                    if positive(count := t.counted(NT if norm_in else 1, (1 - RING) * (NT if norm_in else 1))):
                        sp.wait_ge(in_normed if norm_in else xt_done, count)
                    sp.dma_start(m.x_in[:, t.r], t.of(x_v)).then_inc(x_loaded[t.r], 16)
                b = t.back(4 + lag)
                if b.there():
                    if positive(count := b.counted(1, 1 - RING)):
                        sp.wait_ge(summed, count)
                    sp.dma_start(m.x_res[:, b.r], b.of(x_v)).then_inc(res_loaded[b.r], 16)
                b = t.back(1 + lag)
                if b.there():
                    sp.wait_ge(loaded_first, 16 * 3)
                    sp.wait_ge(k_copied, b.counted(1, 1))
                    if positive(count := b.counted(H, (1 - RING) * H)):
                        sp.wait_ge(exp_scored, count)
                    if b.i is None and b.c == 0:
                        sp.wait_ge(cleared, CLEARED)
                    for g in range(GH):
                        q = slice(ROWS * g, ROWS * g + ROWS)
                        sp.dma_start(m.k_blocks[q, b.r, :, g, :].bitcast(F32), m.k_stack[q].bitcast(F32)).then_inc(blocks_loaded[b.r], 16)
                b = t.back(5 + lag)
                if b.there():
                    sp.wait_ge(y_done if norm_out else summed, b.counted(NT, NT) if norm_out else b.counted(1, 1))
                    sp.dma_start(b.of(y_v), m.y_out[:, b.r]).then_inc(stored[b.r], 16)

            run_turns(sp, step, first, B, B + 5 + lag)
            for r in range(RING):
                sp.wait_ge(stored[r], 16 * len(range(r, B, RING)))

        @block.gpsimd
        def _(pool):
            pool.dma_start(m.sel[:, :, 0:parts].rearrange("p w a g c -> p w (a g c)"), w["sel"].rearrange("p (w c) -> p w c", w=2).bitcast(F32R)).then_inc(sel_loaded, 16)
            v_flat = m.v_ones.rearrange("p r t h c -> p (r t h) c")
            pool.memset(v_flat, 0.0).then_inc(v_cleared, 1)
            pool.wait_ge(v_cleared, 1)
            pool.memset(v_flat[:, :, hd:hd + 1], 1.0).then_inc(v_cleared, 1)
            pool.memset(m.max_rows[:], 0.0).then_inc(cleared, 1)
            pool.memset(m.neg_half[:], -0.5).then_inc(cleared, 1)
            if clear_blocks:
                pool.memset(m.k_blocks[:].bitcast(F32), 0.0).then_inc(cleared, 1)
            pool.wait_ge(cleared, CLEARED)
            pool.wait_ge(loaded, LOADED)

            def step(t):
                if norm_in and t.there():
                    pool.wait_ge(in_eps, t.counted(1, 1))
                    pool.tensor_tensor(m.rstd_in[:], m.var_eps_in[:], m.neg_half[:], ALU.pow).then_inc(in_rstd, 1)
                    pool.wait_ge(in_normed, t.counted(NT, NT))
                    xn = m.x_norm[:, t.r]
                    pool.tensor_tensor(xn, xn, m.wide[:, 1:2, :].to_broadcast([P, NT, D]), ALU.mult).then_inc(in_scaled, 1)
                    pool.wait_ge(in_scaled, t.counted(1, 1))
                    pool.tensor_tensor(xn, xn, m.wide[:, 2:3, :].to_broadcast([P, NT, D]), ALU.add).then_inc(in_ready, 1)
                b = t.back(3 + lag)
                if b.there():
                    res = m.x_res[:, b.r]
                    pool.wait_ge(res_loaded[b.r], b.used(16))
                    pool.tensor_tensor(res, res, m.wide[:, 0:1, :].to_broadcast([P, NT, D]), ALU.add).then_inc(bias_added, 1)
                    if norm_out:
                        pool.wait_ge(eps_done, b.counted(1, 1))
                        pool.tensor_tensor(m.rstd[:], m.var_eps[:], m.neg_half[:], ALU.pow).then_inc(rstd_done, 1)

            run_turns(pool, step, first, B, total)

        @block.tensor
        def _(pe):
            def weigh(b, group):
                pe.wait_ge(exp_done, b.counted(H, GH * group + GH))
                if group == 0:
                    pe.wait_ge(v_copied, b.counted(NT, NT))
                if group % 2 == 0:
                    if positive(count := b.counted(2, group // 2)):
                        pe.wait_ge(out_copied, count)
                for kt in range(NT):
                    for g in range(GH):
                        h = GH * group + g
                        lhs = m.v_ones[:, b.r, kt, h, :]
                        if causal and kt == 1:
                            rhs, q0 = m.probs[:, h % (2 * GH), S:S + P], P
                        else:
                            rhs, q0 = m.probs[:, h % (2 * GH), kt * S:kt * S + S], 0
                        ins = pe.matmul(ps_out[ROWS * g:ROWS * g + ROWS, group % 2, q0:S], lhs, rhs, start=(kt == 0), stop=(kt == NT - 1))
                ins.then_inc(weighed, 1)

            def score_for_exp(b, h):
                if h == 0:
                    pe.wait_ge(shifted, b.counted(1, 1))
                n = b.counted(H, h - 1)
                if positive(count := n):
                    pe.wait_ge(exp_done, count)
                G, g = divmod(h, GH)
                bank = ps_exp[:, h % 2, :]
                for kt in range(NT):
                    keys = m.k_blocks[:, b.r, G, g, kt * P:kt * P + P]
                    if causal and kt == 1:
                        ins = pe.matmul(bank[:, S:S + P], keys, m.q_shift[:, b.r, G, P:S], start=False, stop=False, skip_group_check=True)
                    else:
                        ins = pe.matmul(bank[:, kt * S:kt * S + S], keys, m.q_shift[:, b.r, G, :], start=(kt == 0), stop=not causal, skip_group_check=True)
                if causal:
                    out = bank.rearrange("p (a c) -> p a c", a=2)[:, :, 0:P]
                    ins = pe.matmul(out, m.ident_bf[:], m.mask[:, 1, 0:NT, :], start=False, stop=True, skip_group_check=True)
                ins.then_inc(exp_scored, 1)

            def score_for_max(b, n):
                G, o = divmod(n, len(max_ops))
                qt, heads, keys = max_ops[o]
                if n == 0:
                    pe.wait_ge(q_copied, b.counted(1, 1))
                    pe.wait_ge(blocks_loaded[b.r], b.used(16 * GH))
                if positive(count := b.counted(KM, n - 1)):
                    pe.wait_ge(max_done, count)
                queries = m.q_stack[:, b.r, G, qt * P:qt * P + P]
                bank = ps_max[:, n % 2, :]
                ins = pe.matmul(bank, queries, m.k_blocks[:, b.r, G, heads, keys], start=True, stop=not causal, skip_group_check=True)
                if causal and qt == 0:
                    ins = pe.matmul(bank, m.ident_bf[:], m.mask[:, 0, :, :], start=False, stop=True, skip_group_check=True)
                if causal and qt == 1:
                    out = bank.rearrange("p (h k) -> p h k", h=2)[:, :, P:S]
                    ins = pe.matmul(out, m.ident_bf[:], m.mask[:, 0, 0:2, :], start=False, stop=True, skip_group_check=True)
                ins.then_inc(max_scored, 1)

            def turn_max(b):
                pe.wait_ge(rows_ready, b.counted(1, 1))
                if positive(count := b.counted(1, -1)):
                    pe.wait_ge(divided, count)
                pe.wait_ge(q_copied, b.counted(1, 2))
                for G in range(NG):
                    for qt in range(NT):
                        ins = pe.transpose(ps_wide[:, G, qt * P:qt * P + P], m.max_rows[:, qt, GH * G:GH * G + GH, :], m.ident[:])
                ins.then_inc(max_turned, 1)

            def stack(b, which, done):
                for G in range(NG):
                    for part in range(parts):
                        src = (m.qk_hi, m.qk_lo)[part] if parts == 2 else m.qk_lo
                        ins = pe.matmul(ps_wide[:, G, :], m.sel[:, which, part, G, :], src[:, which, :], start=(part == 0), stop=(part == parts - 1),
                                        skip_group_check=True)
                ins.then_inc(done, 1)

            def step(t):
                prep, mx, ex, tail = t.back(lag), t.back(1 + lag), t.back(2 + lag), t.back(3 + lag)
                if mx.i is None and mx.c == 0:
                    pe.wait_ge(const_ready, 3 + (HD < D))
                for s in range(H):
                    if s == at["project_v"] and prep.i is None and prep.c == 0:
                        pe.wait_ge(loaded, LOADED)
                        pe.wait_ge(sel_loaded, 16)
                    if mx.there() and 0 <= s - MAX_FROM < KM:
                        score_for_max(mx, s - MAX_FROM)
                    if s == at["turn_max"] and ex.there():
                        turn_max(ex)
                    if s < 4 and tail.there():
                        score_for_exp(tail, 12 + s)
                    if s >= 4 and ex.there():
                        score_for_exp(ex, s - 4)
                    if s == 1 and tail.there():
                        weigh(tail, 2)
                    if s == 5 and tail.there():
                        weigh(tail, 3)
                    if s == 9 and ex.there():
                        weigh(ex, 0)
                    if s == 13 and ex.there():
                        weigh(ex, 1)
                    if s == at["turn_x"] and prep.there():
                        if norm_in:
                            pe.wait_ge(in_ready, prep.counted(1, 1))
                        else:
                            pe.wait_ge(x_loaded[prep.r], prep.used(16))
                        if positive(count := prep.counted(1, -3)):
                            pe.wait_ge(summed, count)
                        src = m.x_norm if norm_in else m.x_in
                        for tile in range(NT):
                            ins = pe.transpose(ps_small[:, 0, tile * P:tile * P + P], src[:, prep.r, tile, :], m.ident[:])
                        ins.then_inc(xt_done, 1)
                    if s == at["project_qk"] and prep.there():
                        pe.wait_ge(xt_copied, prep.counted(1, 1))
                        for which in range(2):
                            ins = pe.matmul(ps_small[:, which, :], m.w_qk[:, which, :], m.x_t[:], start=True, stop=True)
                        ins.then_inc(qk_done, 1)
                    if s == at["project_v"] and prep.there():
                        pe.wait_ge(lo_ready, prep.counted(1, 1))
                        for tile in range(NT):
                            out = ps_small[:, 0, tile * HD:tile * HD + HD]
                            ins = pe.matmul(out, m.x_t[:, tile * P:tile * P + P], m.w_v[:, 0:HD], start=True, stop=(hd == 4))
                            if hd == 8:
                                ins = pe.matmul(out, m.rows_f32[:, 1, :], m.rows_f32[:, 0, 0:HD], start=False, stop=True)
                        ins.then_inc(v_done, 1)
                    if s == at["turn_out"] and tail.there():
                        pe.wait_ge(out_copied, tail.counted(2, 2))
                        pe.wait_ge(shifted, tail.counted(1, 2))
                        for G in range(NG):
                            for qt in range(NT):
                                ins = pe.transpose(ps_wide.rearrange("p g s -> p (g s)")[:, (qt * NG + G) * P:(qt * NG + G + 1) * P],
                                                   m.out_t[:, G, qt * P:qt * P + P], m.ident[:])
                        ins.then_inc(out_turned, 1)
                    if s == at["stack_k"] and prep.there():
                        pe.wait_ge(lo_ready, prep.counted(1, 1))
                        if positive(count := prep.counted(1, -2)):
                            pe.wait_ge(divided, count)
                        stack(prep, 1, k_stacked)
                    if s == at["stack_q"] and prep.there():
                        pe.wait_ge(k_copied, prep.counted(1, 1))
                        stack(prep, 0, q_stacked)
                    if s == at["turn_norm"] and tail.there():
                        pe.wait_ge(divided, tail.counted(1, 1))
                        pe.wait_ge(v_copied, tail.counted(NT, 4 * NT))
                        for qt in range(NT):
                            ins = pe.transpose(ps_small[:, 1, qt * P:qt * P + P], m.out_n[:, qt, :], m.ident[:])
                        ins.then_inc(norm_turned, 1)
                    if s == at["project_out"] and tail.there():
                        pe.wait_ge(norm_copied, tail.counted(1, 1))
                        for qt in range(NT):
                            ins = pe.matmul(ps_small[:, 0, qt * D:qt * D + D], m.out_nt[0:HD, qt * P:qt * P + P], m.w_o[0:HD, :], start=True, stop=True)
                        ins.then_inc(projected, 1)

            pe.wait_ge(loaded_first, 16 * 3)
            run_turns(pe, step, first, B, total)

        @block.scalar
        def _(act):
            def exp(b, h):
                act.wait_ge(exp_scored, b.counted(H, h + 1))
                if positive(count := b.counted(NG, h // GH - 1)):
                    act.wait_ge(weighed, count)
                act.activation(m.probs[:, h % (2 * GH), 0:EW], exp_cols(h), ACT.Exp, scale=SCALE).then_inc(exp_done, 1)

            def exp_cols(h):
                return ps_exp[:, h % 2, 0:EW]

            def copy_out(b, half):
                act.wait_ge(weighed, b.counted(NG, 2 * half + 2))
                if half == 0:
                    if positive(count := b.counted(1, 0)):
                        act.wait_ge(out_turned, count)
                act.activation(m.out_t[:, 2 * half:2 * half + 2, :], ps_out[:], ACT.Copy).then_inc(out_copied, 1)

            def step(t):
                prep, ex, tail = t.back(lag), t.back(2 + lag), t.back(3 + lag)
                for s in range(H):
                    if s < 4 and tail.there():
                        exp(tail, 12 + s)
                    if s >= 4 and ex.there():
                        exp(ex, s - 4)
                    if s == at["copy_x"] and prep.there():
                        act.wait_ge(xt_done, prep.counted(1, 1))
                        if positive(count := prep.counted(1, 0)):
                            act.wait_ge(v_done, count)
                        act.activation(m.x_t[:], ps_small[:, 0, :], ACT.Copy).then_inc(xt_copied, 1)
                    if s == at["copy_hi"] and prep.there():
                        act.wait_ge(qk_done, prep.counted(1, 1))
                        if positive(count := prep.counted(1, 0)):
                            act.wait_ge(q_stacked, count)
                        for which in range(2):
                            act.activation(m.qk_hi[:, which, :], ps_small[:, which, :], ACT.Identity, bias=m.col[:, which:which + 1]).then_inc(hi_ready, 1)
                    if s == at["copy_out_1"] and tail.there():
                        copy_out(tail, 1)
                    if s == at["copy_v"] and prep.there():
                        act.wait_ge(v_done, prep.counted(1, 1))
                        if positive(count := prep.counted(NG, (1 - RING) * NG)):
                            act.wait_ge(weighed, count)
                        for tile in range(NT):
                            src = ps_small[:, 0, tile * HD:tile * HD + HD].rearrange("p (h d) -> p h d", h=H)
                            act.activation(m.v_ones[:, prep.r, tile, :, 0:hd], src, ACT.Copy).then_inc(v_copied, 1)
                    if s == at["copy_k"] and prep.there():
                        act.wait_ge(k_stacked, prep.counted(1, 1))
                        if prep.i is not None or prep.c > 0:
                            p = prep.back(1)
                            act.wait_ge(blocks_loaded[p.r], p.used(16 * GH))
                        act.activation(m.k_stack[:], ps_wide[:], ACT.Identity, bias=m.col[:, 2:3]).then_inc(k_copied, 1)
                    if s == at["copy_q"] and prep.there():
                        act.wait_ge(q_stacked, prep.counted(1, 1))
                        if positive(count := prep.counted(1, 1 - RING)):
                            act.wait_ge(shifted, count)
                        act.activation(m.q_stack[:, prep.r], ps_wide[:], ACT.Copy).then_inc(q_copied, 1)
                    if s == at["copy_norm"] and tail.there():
                        act.wait_ge(norm_turned, tail.counted(1, 1))
                        if positive(count := tail.counted(1, 0)):
                            act.wait_ge(projected, count)
                        act.activation(m.out_nt[0:HD, :], ps_small[0:HD, 1, :], ACT.Copy).then_inc(norm_copied, 1)
                    if s == at["copy_out_0"] and ex.there():
                        copy_out(ex, 0)

            for dst, src in later:
                act.dma_start(dst, src).then_inc(loaded, 16)
            act.wait_ge(loaded_first, 16 * 3)
            act.wait_ge(v_cleared, 2)
            run_turns(act, step, first, B, total)

        @block.vector
        def _(dve):
            if HD < D:
                dve.memset(m.out_n[:, :, HD:D], 0.0).then_inc(const_ready, 1)
            dve.wait_ge(loaded_first, 16 * 3)
            dve.tensor_copy(m.ident_bf[:], m.ident[:]).then_inc(const_ready, 1)
            dve.wait_ge(loaded, LOADED)
            for which in range(2):
                src = m.mask_f32[:, which:which + 1, :].to_broadcast([P, GH, P])
                dve.tensor_copy(m.mask[:, which], src).then_inc(const_ready, 1)
            dve.wait_ge(cleared, 2)

            def reduce(b, n):
                G, o = divmod(n, len(max_ops))
                qt, heads, keys = max_ops[o]
                nh, nk = heads.stop - heads.start, keys.stop - keys.start
                dve.wait_ge(max_scored, b.counted(KM, n + 1))
                if n == 0:
                    if positive(count := b.counted(1, 0)):
                        dve.wait_ge(rows_ready, count)
                dve.tensor_reduce(m.neg_max[:, qt, GH * G + heads.start:GH * G + heads.stop],
                                  ps_max[:, n % 2, :].rearrange("p (h k) -> p h k", h=nh), AX.X, ALU.max, negate=True).then_inc(max_done, 1)

            def split_max(b):
                dve.wait_ge(max_done, b.counted(KM, KM))
                if positive(count := b.counted(1, 0)):
                    dve.wait_ge(max_turned, count)
                dve.tensor_copy(m.max_rows[:, :, :, row_hi].bitcast(F32R), m.neg_max[:]).then_inc(max_hi, 1)
                dve.wait_ge(max_hi, b.counted(1, 1))
                dve.tensor_tensor(m.max_rows[:, :, :, row_lo].bitcast(F32R), m.neg_max[:], m.max_rows[:, :, :, row_hi], ALU.subtract).then_inc(rows_ready, 1)

            def norm(b, src, dst, stats, mean_var, var_eps, rstd, sems, part):
                s_stats, s_aggr, s_eps, s_rstd, s_done = sems
                if part == 0:
                    if positive(count := b.counted(NT, 0)):
                        dve.wait_ge(s_done, count)
                    for tile in range(NT):
                        dve.bn_stats(stats[:, tile, :], src[:, tile, :]).then_inc(s_stats, 1)
                    dve.wait_ge(s_stats, b.counted(NT, NT))
                    dve.tensor_copy(mean_var[:, NT, 0:1], stats[:, 0, 1:2]).then_inc(s_aggr, 1)
                    for tile in range(NT):
                        dve.bn_aggr(mean_var[:, tile, :], stats[:, tile, :]).then_inc(s_aggr, 1)
                    dve.wait_ge(s_aggr, b.counted(NT + 1, NT + 1))
                    dve.tensor_scalar(var_eps[:], mean_var[:, 0:NT, 1], EPS, None, ALU.add).then_inc(s_eps, 1)
                else:
                    dve.wait_ge(s_rstd, b.counted(1, 1))
                    for tile in range(NT):
                        dve.tensor_scalar(dst[:, tile, :], src[:, tile, :], mean_var[:, tile, 0:1], rstd[:, tile:tile + 1],
                                          ALU.subtract, ALU.mult).then_inc(s_done, 1)

            def step(t):
                prep, mx, ex, tail = t.back(lag), t.back(1 + lag), t.back(2 + lag), t.back(3 + lag)
                for s in range(H):
                    if mx.there() and 0 <= s - MAX_FROM < KM:
                        reduce(mx, s - MAX_FROM)
                    if mx.there() and s == MAX_FROM + KM - 1:
                        split_max(mx)
                    if norm_in and t.there() and s in (at["in_stats"], at["in_norm"]):
                        if s == at["in_stats"]:
                            dve.wait_ge(x_loaded[t.r], t.used(16))
                        else:
                            if positive(count := t.counted(1, 1 - RING)):
                                dve.wait_ge(xt_done, count)
                        norm(t, m.x_in[:, t.r], m.x_norm[:, t.r], m.stats_in, m.mean_var_in, m.var_eps_in, m.rstd_in,
                             (in_stats, in_aggr, in_eps, in_rstd, in_normed), 0 if s == at["in_stats"] else 1)
                    if s == at["shift"] and ex.there():
                        dve.wait_ge(max_turned, ex.counted(1, 1))
                        if positive(count := ex.counted(H, (1 - RING) * H)):
                            dve.wait_ge(exp_scored, count)
                        dve.tensor_tensor(m.q_shift[:, ex.r], m.q_stack[:, ex.r].bitcast(F32), ps_wide[:], ALU.add).then_inc(shifted, 1)
                    if s == at["split_lo"] and prep.there():
                        dve.wait_ge(hi_ready, prep.counted(2, 2))
                        if positive(count := prep.counted(1, 0)):
                            dve.wait_ge(q_stacked, count)
                        if parts == 1:
                            dve.scalar_tensor_tensor(m.qk_lo[:], m.qk_hi[:].bitcast(F32), m.col[:, 3:4], ps_small[:], ALU.mult, ALU.add).then_inc(lo_ready, 1)
                        else:
                            for which in range(2):
                                ins = dve.scalar_tensor_tensor(m.qk_lo[:, which, :], ps_small[:, which, :], m.col[:, which:which + 1],
                                                               m.qk_hi[:, which, :].bitcast(F32), ALU.add, ALU.subtract)
                            ins.then_inc(lo_ready, 1)
                    if s == at["divide"] and tail.there():
                        dve.wait_ge(out_turned, tail.counted(1, 1))
                        turned = ps_wide.rearrange("p g s -> p (g s)").rearrange("p (t h c) -> p t h c", t=NT, h=H)
                        if positive(count := tail.counted(1, 0)):
                            dve.wait_ge(divided, count)
                        dve.reciprocal(m.inv_sum[:], turned[:, :, :, hd]).then_inc(inv_done, 1)
                        dve.wait_ge(inv_done, tail.counted(1, 1))
                        if positive(count := tail.counted(1, 0)):
                            dve.wait_ge(norm_turned, count)
                        out = m.out_n[:, :, 0:HD].rearrange("p t (h d) -> p t h d", h=H)
                        dve.tensor_tensor(out, turned[:, :, :, 0:hd], m.inv_sum[:].unsqueeze(3).to_broadcast([P, NT, H, hd]), ALU.mult).then_inc(divided, 1)
                    if s == at["add_out"] and tail.there():
                        dve.wait_ge(projected, tail.counted(1, 1))
                        dve.wait_ge(bias_added, tail.counted(1, 1))
                        if not norm_out and (tail.i is not None or tail.c >= RING):
                            dve.wait_ge(stored[tail.r], tail.back(RING).used(16))
                        if norm_out:
                            if positive(count := tail.counted(NT, 0)):
                                dve.wait_ge(y_done, count)
                        dst = m.y[:] if norm_out else m.y_out[:, tail.r]
                        dve.tensor_tensor(dst, ps_small[:, 0, :].rearrange("p (t d) -> p t d", t=NT), m.x_res[:, tail.r], ALU.add).then_inc(summed, 1)
                        if norm_out:
                            dve.wait_ge(summed, tail.counted(1, 1))
                            norm(tail, m.y, None, m.stats, m.mean_var, m.var_eps, m.rstd,
                                 (stats_done, aggr_done, eps_done, rstd_done, y_done), 0)
                    if s == at["norm_out"] and tail.there() and norm_out:
                        if tail.i is not None or tail.c >= RING:
                            dve.wait_ge(stored[tail.r], tail.back(RING).used(16))
                        norm(tail, m.y, m.y_out[:, tail.r], m.stats, m.mean_var, m.var_eps, m.rstd,
                             (stats_done, aggr_done, eps_done, rstd_done, y_done), 1)

            run_turns(dve, step, first, B, total)


SLOTS_1 = {"split": (10, 17, 17, 17), "stats": 0, "norm": 3, "turn_x": 8, "route": 11, "turn_y": 12, "norm_y": 15, "score": 14, "weigh": 16, "turn_gates": 19}
SLOTS_2 = {"split": (2, 12, 12, 12), "stats": 0, "norm": 0, "turn_x": 0, "route": 1, "score": 2, "turn_y": 4, "rank": 6, "weigh": 11, "turn_gates": 12, "norm_y": 12}


class Links:

    def __init__(self, turn, per):
        self.turn, self.per, self.n = turn, per, 0

    def next(self):
        self.n += 1
        assert self.n <= self.per
        return self.turn.counted(self.per, self.n)


BT = 4
TOK = BT * P
NB = B * S // TOK
BRING = 2
LO = 32


def expert_stage(nc, tag, experts, chunks, last_rows, gated, slots, x, x_more, y, w):
    E = experts
    x_v = x.rearrange("b s d -> (b s) d").rearrange("(n t p) d -> n p t d", p=P, t=BT)
    more_v = None if x_more is None else x_more.rearrange("b s d -> (b s) d").rearrange("(n t p) d -> n p t d", p=P, t=BT)
    y_v = y.rearrange("b s d -> (b s) d").rearrange("(n t p) d -> n p t d", p=P, t=BT)
    norm_in = x_more is not None
    NX = 2 if norm_in else 1
    first = 4
    BEHIND = 2
    NW = 2 if gated else 1
    gates = chunks - 1 if gated else E
    per_gate = chunks // E if not gated else 1
    CHAIN = 27 if gated else 13
    SCALED = gates if gated else chunks

    def place(c):
        return 4 if gated and c == gates else c % 4

    def place_used(c):
        if gated and c == gates:
            return c - chunks
        return c - 4 if c >= 4 or not gated else c - 4 - 1

    def bank(b, c):
        return (b.r * chunks + c) % 2

    with ExitStack() as ctx:
        sem = stage_semaphores(nc, ctx, tag)

        def sb(name, shape, dt=F32):
            return ctx.enter_context(nc.sbuf_tensor(f"{tag}_{name}", shape, dt))

        def psum(name, shape):
            return ctx.enter_context(nc.psum_tensor(f"{tag}_{name}", shape, F32))

        w_raw = sb("w_raw", [P, chunks, NW, P])
        w_hi = sb("w_hi", [P, chunks, NW, P], F32R)
        w_lo = sb("w_lo", [P, chunks, NW, P], F32R)
        w_out = sb("w_out", [P, chunks, D])
        w_gate = sb("w_gate", [P, E])
        b_out = sb("b_out", [P, D])
        b_hidden = sb("b_hidden", [P, chunks])
        wide = sb("wide", [P, 2, D])
        gate_bias = sb("gate_bias", [P, E])
        before = sb("before", [P, E, E])
        ident = sb("ident", [P, P])
        sel = sb("sel", [P, gates, P], F32R)
        neg_half = sb("neg_half", [P, BT])
        x_in = sb("x_in", [P, BRING, BT, D])
        x_res = sb("x_res", [P, 2, BRING, BT, D])
        x_norm = sb("x_norm", [P, BT, D])
        x_t = sb("x_t", [P, TOK])
        x_hi = sb("x_hi", [P, BRING, TOK], F32R)
        x_lo = sb("x_lo", [P, BRING, TOK], F32R)
        gate_t = sb("gate_t", [P, BRING, TOK], F32R)
        gate_rows = sb("gate_rows", [P, BT, P])
        hidden = sb("hidden", [P, 5, TOK])
        scaled = sb("scaled", [P, 5, TOK])
        mixed = sb("mixed", [P, 4, TOK])
        y_t = sb("y_t", [P, TOK])
        y_sum = sb("y_sum", [P, BT, D])
        y_out = sb("y_out", [P, BRING, BT, D])
        stats = sb("stats", [P, 2, BT, 6])
        mean_var = sb("mean_var", [P, 2, BT + 1, 2])
        var_eps = sb("var_eps", [P, 2, BT])
        rstd = sb("rstd", [P, 2, BT])
        logits = sb("logits", [P, BT, E])
        greater = sb("greater", [P, BT, E, E])
        equal = sb("equal", [P, BT, E, E])
        rank = sb("rank", [P, BT, E])
        chosen = sb("chosen", [P, BT, E])
        shifted = sb("shifted", [P, BT, E])
        weight = sb("weight", [P, BT, E])
        top = sb("top", [P, BT])
        total_w = sb("total_w", [P, BT])
        small = sb("small", [P, 8, BT, 4, 2])
        group_sums = sb("group_sums", [P, BT * 4])
        group_ranks = sb("group_ranks", [P, BT * 4])

        ps_h = psum("ps_h", [P, 2 * NW, TOK])
        ps_gate = psum("ps_gate", [P, 1 if gated else 2, TOK])
        ps_y = psum("ps_y", [P, TOK])
        ps_turn = psum("ps_turn", [P, TOK])
        ps_logits = psum("ps_logits", [P, BT, E])
        GR = 1 if gated else 2

        sel_loaded, loaded_first, loaded, cleared = sem("sel_loaded"), sem("loaded_first"), sem("loaded"), sem("cleared")
        raw_loaded = [sem(f"raw_loaded{n}") for n in range(4)]
        raw_hi, raw_split, second_loaded = sem("raw_hi"), sem("raw_split"), sem("second_loaded")
        x_loaded = [sem(f"x_loaded{r}") for r in range(BRING)]
        res_loaded = [sem(f"res_loaded{r}") for r in range(BRING)]
        stored = [sem(f"stored{r}") for r in range(BRING)]
        xt_done, routed, gates_turned = sem("xt_done"), sem("routed"), sem("gates_turned")
        first_done, spread, second_done = sem("first_done"), sem("spread"), sem("second_done")
        y_turned = sem("y_turned")
        xt_copied, hi_ready, score_done, gates_copied = sem("xt_copied"), sem("hi_ready"), sem("score_done"), sem("gates_copied")
        activated, y_copied = sem("activated"), sem("y_copied")
        lo_ready, to_score, rows_ready = sem("lo_ready"), sem("to_score"), sem("rows_ready")
        mixed_done, scaled_done, chained = sem("mixed_done"), sem("scaled_done"), sem("chained")
        in_stats, in_aggr, in_eps, in_normed = sem("in_stats"), sem("in_aggr"), sem("in_eps"), sem("in_normed")
        summed, out_stats, out_aggr, out_eps, y_done = sem("summed"), sem("out_stats"), sem("out_aggr"), sem("out_eps"), sem("y_done")
        in_rstd, in_scaled, in_ready = sem("in_rstd"), sem("in_scaled"), sem("in_ready")
        res_ready, out_rstd = sem("res_ready"), sem("out_rstd")

        block = ctx.enter_context(nc.Block())

        PIECE = -(-chunks // 4)
        pieces = [range(c, min(c + PIECE, chunks)) for c in range(0, chunks, PIECE)]

        def piece_of(weights, n):
            return weights[:, pieces[n].start:pieces[n].stop].rearrange("p c w f -> p (c w) f")

        later = [(w_gate[:], w["gate"]), (before[:], w["before"]), (gate_bias[:], w["gate_bias"]), (b_hidden[:], w["b_hidden"]),
                 (b_out[:], w["b_out"])]
        LOADED = 16 * len(later)

        @block.sync
        def _(sp):
            for dst, src in ((ident[:], w["ident"]), (wide[:], w["wide"])):
                sp.dma_start(dst, src).then_inc(loaded_first, 16)

            def io_step(t):
                if t.there():
                    if norm_in:
                        if positive(count := t.counted(BT, (1 - BRING) * BT)):
                            sp.wait_ge(in_normed, count)
                    else:
                        if positive(count := t.counted(1, 1 - BRING)):
                            sp.wait_ge(xt_done, count)
                    sp.dma_start(x_in[:, t.r], t.of(x_v)).then_inc(x_loaded[t.r], 16)
                b = t.back(2)
                if b.there():
                    if positive(count := b.counted(1, 1 - BRING)):
                        sp.wait_ge(summed, count)
                    sp.dma_start(x_res[:, 0, b.r], b.of(x_v)).then_inc(res_loaded[b.r], 16)
                    if norm_in:
                        sp.dma_start(x_res[:, 1, b.r], b.of(more_v)).then_inc(res_loaded[b.r], 16)
                b = t.back(3)
                if b.there():
                    sp.wait_ge(y_done, b.counted(BT, BT))
                    sp.dma_start(b.of(y_v), y_out[:, b.r]).then_inc(stored[b.r], 16)

            run_turns(sp, io_step, first, NB, NB + 3, BRING)
            for r in range(BRING):
                sp.wait_ge(stored[r], 16 * len(range(r, NB, BRING)))

        @block.gpsimd
        def _(pool):
            pool.dma_start(sel[:], w["sel"].bitcast(F32R)).then_inc(sel_loaded, 16)
            pool.memset(neg_half[:], -0.5).then_inc(cleared, 1)
            pool.memset(gate_rows[:], 0.0).then_inc(cleared, 1)
            pool.wait_ge(cleared, 2)
            pool.wait_ge(loaded_first, 16 * 2)

            def step(t):
                if norm_in and t.there():
                    pool.wait_ge(in_eps, t.counted(1, 1))
                    pool.tensor_tensor(rstd[:, 0], var_eps[:, 0], neg_half[:], ALU.pow).then_inc(in_rstd, 1)
                    pool.wait_ge(in_normed, t.counted(BT, BT))
                    pool.tensor_tensor(x_norm[:], x_norm[:], wide[:, 0:1, :].to_broadcast([P, BT, D]), ALU.mult).then_inc(in_scaled, 1)
                    pool.wait_ge(in_scaled, t.counted(1, 1))
                    pool.tensor_tensor(x_norm[:], x_norm[:], wide[:, 1:2, :].to_broadcast([P, BT, D]), ALU.add).then_inc(in_ready, 1)
                b = t.back(2)
                if b.there():
                    if norm_in:
                        pool.wait_ge(res_loaded[b.r], b.used(16 * NX))
                        pool.tensor_tensor(x_res[:, 0, b.r], x_res[:, 0, b.r], x_res[:, 1, b.r], ALU.add).then_inc(res_ready, 1)
                    pool.wait_ge(out_eps, b.counted(1, 1))
                    pool.tensor_tensor(rstd[:, 1], var_eps[:, 1], neg_half[:], ALU.pow).then_inc(out_rstd, 1)

            run_turns(pool, step, first, NB, NB + 2, BRING)

        @block.tensor
        def _(pe):
            def first_products(b, c):
                if c == 0:
                    pe.wait_ge(lo_ready, b.counted(1, 1))
                if gated:
                    if positive(count := b.counted(chunks, c - 1)):
                        pe.wait_ge(mixed_done, count)
                else:
                    if positive(count := b.counted(chunks, c - 1)):
                        pe.wait_ge(activated, count)
                if b.i is None and b.c == 0 and c % PIECE == 0:
                    pe.wait_ge(raw_split, c // PIECE + 1)
                rows = P if c < chunks - 1 else last_rows
                for k in range(NW):
                    out = ps_h[0:rows, NW * bank(b, c) + k, :]
                    pe.matmul(out, w_hi[:, c, k, 0:rows], x_hi[:, b.r], start=True, stop=False)
                    pe.matmul(out, w_hi[:, c, k, 0:rows], x_lo[:, b.r], start=False, stop=False)
                    ins = pe.matmul(out, w_lo[:, c, k, 0:rows], x_hi[:, b.r], start=False, stop=True)
                ins.then_inc(first_done, 1)

            def spread_gate(b, g):
                if g == 0:
                    pe.wait_ge(gates_copied, b.counted(1, 1))
                if gated:
                    if positive(count := b.counted(SCALED, g)):
                        pe.wait_ge(scaled_done, count)
                else:
                    if positive(count := b.counted(chunks, (g - 1) * per_gate)):
                        pe.wait_ge(scaled_done, count)
                pe.matmul(ps_gate[:, g % GR, :], sel[:, g, :], gate_t[:, b.r], start=True, stop=True).then_inc(spread, 1)

            def second_product(b, c):
                if c == 0:
                    if positive(count := b.counted(1, 0)):
                        pe.wait_ge(y_copied, count)
                    if b.i is None and b.c == 0:
                        pe.wait_ge(second_loaded, 16)
                    if not gated:
                        pe.matmul(ps_y[:], b_out[:], gate_t[:, b.r].bitcast(F32), start=True, stop=False)
                if gated and c == gates:
                    pe.wait_ge(mixed_done, b.counted(chunks, c + 1))
                else:
                    pe.wait_ge(scaled_done, b.counted(SCALED, c + 1))
                rows = P if c < chunks - 1 else last_rows
                ins = pe.matmul(ps_y[:], w_out[0:rows, c, :], scaled[0:rows, place(c), :], start=(gated and c == 0), stop=(c == chunks - 1))
                ins.then_inc(second_done, 1)

            def step(t):
                new, cur, old = t, t.back(1), t.back(2)
                for s in range(chunks):
                    if cur.there():
                        if gated:
                            first_products(cur, s)
                            if s > 0:
                                spread_gate(cur, s - 1)
                        else:
                            if s % per_gate == 0:
                                spread_gate(cur, s // per_gate)
                            first_products(cur, s)
                    if s < BEHIND and old.there():
                        second_product(old, chunks - BEHIND + s)
                    if s >= BEHIND and cur.there():
                        second_product(cur, s - BEHIND)
                    if s == slots["turn_y"] and old.there():
                        pe.wait_ge(y_copied, old.counted(1, 1))
                        pe.wait_ge(gates_copied, old.counted(1, 2))
                        pe.wait_ge(lo_ready, old.counted(1, 3))
                        for i in range(BT):
                            ins = pe.transpose(ps_turn[:, i * P:i * P + P], y_t[:, i * P:i * P + P], ident[:])
                        ins.then_inc(y_turned, 1)
                    if s == slots["turn_x"] and new.there():
                        if norm_in:
                            pe.wait_ge(in_ready, new.counted(1, 1))
                        else:
                            pe.wait_ge(x_loaded[new.r], new.used(16))
                        if positive(count := new.counted(1, 0)):
                            pe.wait_ge(gates_copied, count)
                        for i in range(BT):
                            src = x_norm[:, i, :] if norm_in else x_in[:, new.r, i, :]
                            ins = pe.transpose(ps_turn[:, i * P:i * P + P], src, ident[:])
                        ins.then_inc(xt_done, 1)
                    if s == slots["route"] and new.there():
                        if new.i is None and new.c == 0:
                            pe.wait_ge(loaded, LOADED)
                            pe.wait_ge(sel_loaded, 16)
                        pe.wait_ge(xt_copied, new.counted(1, 1))
                        for i in range(BT):
                            ins = pe.matmul(ps_logits[:, i, :], x_t[:, i * P:i * P + P], w_gate[:], start=True, stop=True)
                        ins.then_inc(routed, 1)
                    if s == slots["turn_gates"] and new.there():
                        pe.wait_ge(rows_ready, new.counted(1, 1))
                        pe.wait_ge(lo_ready, new.counted(1, 1))
                        if positive(count := new.counted(1, -1)):
                            pe.wait_ge(summed, count)
                        for i in range(BT):
                            ins = pe.transpose(ps_turn[:, i * P:i * P + P], gate_rows[:, i, :], ident[:])
                        ins.then_inc(gates_turned, 1)

            pe.wait_ge(loaded_first, 16 * 2)
            run_turns(pe, step, first, NB, NB + 2, BRING)

        @block.scalar
        def _(act):
            def activate(b, c):
                act.wait_ge(first_done, b.counted(chunks, c + 1))
                rows = P if c < chunks - 1 else last_rows
                if positive(count := b.counted(chunks, place_used(c) + 1)):
                    act.wait_ge(mixed_done if gated else scaled_done, count)
                if gated:
                    act.activation(hidden[0:rows, place(c), :], ps_h[0:rows, NW * bank(b, c), :], ACT.Silu).then_inc(activated, 1)
                else:
                    act.activation(hidden[:, place(c), :], ps_h[:, bank(b, c), :], ACT.Gelu, bias=b_hidden[:, c:c + 1]).then_inc(activated, 1)

            def step(t):
                new, cur, old = t, t.back(1), t.back(2)
                for s in range(chunks):
                    if cur.there():
                        activate(cur, s)
                    if s == BEHIND and old.there():
                        act.wait_ge(second_done, old.counted(chunks, chunks))
                        if positive(count := old.counted(1, 0)):
                            act.wait_ge(y_turned, count)
                        act.activation(y_t[:], ps_y[:], ACT.Copy).then_inc(y_copied, 1)
                    if s == slots["turn_x"] + 1 and new.there():
                        act.wait_ge(xt_done, new.counted(1, 1))
                        if positive(count := new.counted(1, 0)):
                            act.wait_ge(routed, count)
                        act.activation(x_t[:], ps_turn[:], ACT.Copy).then_inc(xt_copied, 1)
                        if positive(count := new.counted(chunks, (1 - BRING) * chunks)):
                            act.wait_ge(first_done, count)
                        act.activation(x_hi[:, new.r], ps_turn[:], ACT.Copy).then_inc(hi_ready, 1)
                    if s == slots["score"] and new.there():
                        if new.i is None and new.c == 0:
                            act.wait_ge(loaded, LOADED)
                        act.wait_ge(to_score, new.counted(1, 1))
                        if gated:
                            act.activation(shifted[:], logits[:], ACT.Sigmoid).then_inc(score_done, 1)
                        else:
                            act.activation(weight[:], shifted[:], ACT.Exp).then_inc(score_done, 1)
                    if s == min(slots["turn_gates"] + 1, chunks - 1) and new.there():
                        act.wait_ge(gates_turned, new.counted(1, 1))
                        if positive(count := new.counted(gates, (1 - BRING) * gates)):
                            act.wait_ge(spread, count)
                        if not gated:
                            if positive(count := new.counted(chunks, (1 - BRING) * chunks)):
                                act.wait_ge(second_done, count)
                        act.activation(gate_t[:, new.r], ps_turn[:], ACT.Copy).then_inc(gates_copied, 1)
                    for n in range(len(pieces)):
                        if s == slots["split"][n] and new.i is None and new.c == 0:
                            act.wait_ge(raw_loaded[n], 16)
                            act.activation(piece_of(w_hi, n), piece_of(w_raw, n), ACT.Copy).then_inc(raw_hi, 1)

            for dst, src in later:
                act.dma_start(dst, src).then_inc(loaded, 16)
            for n in range(len(pieces)):
                act.dma_start(piece_of(w_raw, n), piece_of(w["first"], n)).then_inc(raw_loaded[n], 16)
            act.dma_start(w_out[:], w["second"]).then_inc(second_loaded, 16)
            run_turns(act, step, first, NB, NB + 2, BRING)

        @block.vector
        def _(dve):
            dve.wait_ge(cleared, 2)

            def norm_stats(b, src, k, s_stats, s_aggr, s_eps, s_done):
                if positive(count := b.counted(BT, 0)):
                    dve.wait_ge(s_done, count)
                for i in range(BT):
                    dve.bn_stats(stats[:, k, i, :], src[:, i, :]).then_inc(s_stats, 1)
                dve.wait_ge(s_stats, b.counted(BT, BT))
                dve.tensor_copy(mean_var[:, k, BT, 0:1], stats[:, k, 0, 1:2]).then_inc(s_aggr, 1)
                for i in range(BT):
                    dve.bn_aggr(mean_var[:, k, i, :], stats[:, k, i, :]).then_inc(s_aggr, 1)
                dve.wait_ge(s_aggr, b.counted(BT + 1, BT + 1))
                dve.tensor_scalar(var_eps[:, k], mean_var[:, k, 0:BT, 1], EPS, None, ALU.add).then_inc(s_eps, 1)

            def norm_apply(b, src, dst, k, s_rstd, s_done):
                dve.wait_ge(s_rstd, b.counted(1, 1))
                for i in range(BT):
                    dve.tensor_scalar(dst[:, i, :], src[:, i, :], mean_var[:, k, i, 0:1], rstd[:, k, i:i + 1],
                                      ALU.subtract, ALU.mult).then_inc(s_done, 1)

            def rank_of(values, n, outer, out, links, parts=range(5)):
                shape = [P, outer, n, n]
                gt = greater.rearrange("p t e f -> p (t e f)")[:, 0:outer * n * n].rearrange("p (t e f) -> p t e f", t=outer, e=n)
                eq = equal.rearrange("p t e f -> p (t e f)")[:, 0:outer * n * n].rearrange("p (t e f) -> p t e f", t=outer, e=n)
                others, own = values.unsqueeze(2).to_broadcast(shape), values.unsqueeze(3).to_broadcast(shape)
                if 0 in parts:
                    dve.tensor_tensor(gt, others, own, ALU.is_gt).then_inc(chained, 1)
                    dve.wait_ge(chained, links.next())
                if 1 in parts:
                    dve.tensor_tensor(eq, others, own, ALU.is_equal).then_inc(chained, 1)
                    dve.wait_ge(chained, links.next())
                if 2 in parts:
                    dve.tensor_tensor(eq, eq, before[:, 0:n, 0:n].unsqueeze(1).to_broadcast(shape), ALU.mult).then_inc(chained, 1)
                    dve.wait_ge(chained, links.next())
                if 3 in parts:
                    dve.tensor_tensor(gt, gt, eq, ALU.add).then_inc(chained, 1)
                    dve.wait_ge(chained, links.next())
                if 4 in parts:
                    dve.tensor_reduce(out, gt, AX.X, ALU.add).then_inc(chained, 1)
                    dve.wait_ge(chained, links.next())

            def bc(a):
                return a.unsqueeze(2).to_broadcast([P, BT, E])

            def route_first(b, links):
                if b.i is None and b.c == 0:
                    dve.wait_ge(loaded, LOADED)
                dve.wait_ge(routed, b.counted(1, 1))
                if gated:
                    dve.tensor_copy(logits[:], ps_logits[:]).then_inc(to_score, 1)
                else:
                    dve.tensor_copy(logits[:], ps_logits[:]).then_inc(chained, 1)
                    dve.wait_ge(chained, links.next())
                    rank_of(logits[:], E, BT, rank[:], links)
                    dve.tensor_scalar(chosen[:], rank[:], 2.0, None, ALU.is_lt).then_inc(chained, 1)
                    dve.wait_ge(chained, links.next())
                    dve.tensor_reduce(top[:], logits[:], AX.X, ALU.max).then_inc(chained, 1)
                    dve.wait_ge(chained, links.next())
                    dve.tensor_tensor(shifted[:], logits[:], bc(top[:]), ALU.subtract).then_inc(to_score, 1)

            def col(k):
                return small[:, k].rearrange("p t g a -> p (t g) a")[:, :, 0]

            def route_groups(b, links):
                dve.wait_ge(score_done, b.counted(1, 1))
                dve.tensor_tensor(logits[:], shifted[:], gate_bias[:].unsqueeze(1).to_broadcast([P, BT, E]), ALU.add).then_inc(chained, 1)
                dve.wait_ge(chained, links.next())
                pairs = logits.rearrange("p t (g a c) -> p (t g) a c", g=4, a=2)
                hi, lo = small[:, 0].rearrange("p t g a -> p (t g) a"), small[:, 1].rearrange("p t g a -> p (t g) a")

                dve.tensor_tensor(hi, pairs[:, :, :, 0], pairs[:, :, :, 1], ALU.max)
                dve.tensor_tensor(lo, pairs[:, :, :, 0], pairs[:, :, :, 1], ALU.min).then_inc(chained, 1)
                dve.wait_ge(chained, links.next())
                dve.tensor_tensor(col(2), hi[:, :, 0], hi[:, :, 1], ALU.max)
                dve.tensor_tensor(col(3), hi[:, :, 0], hi[:, :, 1], ALU.min)
                dve.tensor_tensor(col(4), lo[:, :, 0], lo[:, :, 1], ALU.max).then_inc(chained, 1)
                dve.wait_ge(chained, links.next())
                dve.tensor_tensor(col(5), col(3), col(4), ALU.max).then_inc(chained, 1)
                dve.wait_ge(chained, links.next())
                dve.tensor_tensor(group_sums[:], col(2), col(5), ALU.add).then_inc(chained, 1)
                dve.wait_ge(chained, links.next())

            def route_mask(links):
                rank_of(group_sums.rearrange("p (t g) -> p t g", g=4), 4, BT, group_ranks.rearrange("p (t g) -> p t g", g=4), links)
                dve.tensor_scalar(col(6), group_ranks[:], 2.0, None, ALU.is_lt).then_inc(chained, 1)
                dve.wait_ge(chained, links.next())
                dve.tensor_scalar(col(7), col(6), 1.0, -MASKED, ALU.subtract, ALU.mult).then_inc(chained, 1)
                dve.wait_ge(chained, links.next())
                by_group = logits.rearrange("p t (g c) -> p (t g) c", g=4)
                dve.tensor_tensor(by_group, by_group, col(6).unsqueeze(2).to_broadcast([P, BT * 4, 4]), ALU.mult).then_inc(chained, 1)
                dve.wait_ge(chained, links.next())
                dve.tensor_tensor(by_group, by_group, col(7).unsqueeze(2).to_broadcast([P, BT * 4, 4]), ALU.add).then_inc(chained, 1)
                dve.wait_ge(chained, links.next())

            def route_weights(b, links):
                if gated:
                    dve.tensor_scalar(chosen[:], rank[:], 4.0, None, ALU.is_lt).then_inc(chained, 1)
                    dve.wait_ge(chained, links.next())
                    dve.tensor_tensor(weight[:], shifted[:], chosen[:], ALU.mult).then_inc(chained, 1)
                    dve.wait_ge(chained, links.next())
                    dve.tensor_reduce(total_w[:], weight[:], AX.X, ALU.add).then_inc(chained, 1)
                    dve.wait_ge(chained, links.next())
                    dve.tensor_scalar(total_w[:], total_w[:], 1e-20, None, ALU.add).then_inc(chained, 1)
                    dve.wait_ge(chained, links.next())
                    dve.reciprocal(total_w[:], total_w[:]).then_inc(chained, 1)
                    dve.wait_ge(chained, links.next())
                    dve.tensor_tensor(weight[:], weight[:], bc(total_w[:]), ALU.mult).then_inc(chained, 1)
                    dve.wait_ge(chained, links.next())
                    dve.tensor_scalar(weight[:], weight[:], 2.5, None, ALU.mult).then_inc(chained, 1)
                    dve.wait_ge(chained, links.next())
                else:
                    dve.wait_ge(score_done, b.counted(1, 1))
                    dve.tensor_tensor(weight[:], weight[:], chosen[:], ALU.mult).then_inc(chained, 1)
                    dve.wait_ge(chained, links.next())
                    dve.tensor_reduce(total_w[:], weight[:], AX.X, ALU.add).then_inc(chained, 1)
                    dve.wait_ge(chained, links.next())
                    dve.reciprocal(total_w[:], total_w[:]).then_inc(chained, 1)
                    dve.wait_ge(chained, links.next())
                    dve.tensor_tensor(weight[:], weight[:], bc(total_w[:]), ALU.mult).then_inc(chained, 1)
                    dve.wait_ge(chained, links.next())
                if positive(count := b.counted(1, 0)):
                    dve.wait_ge(gates_turned, count)
                dve.tensor_copy(gate_rows[:, :, 0:E].bitcast(F32R), weight[:]).then_inc(chained, 1)
                dve.wait_ge(chained, links.next())
                dve.tensor_tensor(gate_rows[:, :, LO:LO + E].bitcast(F32R), weight[:], gate_rows[:, :, 0:E], ALU.subtract).then_inc(rows_ready, 1)
                assert links.n == CHAIN, links.n

            def scale(b, c):
                dve.wait_ge(activated, b.counted(chunks, c + 1))
                rows = P if c < chunks - 1 else last_rows
                if positive(count := b.counted(chunks, place_used(c) + 1)):
                    dve.wait_ge(second_done, count)
                if gated:
                    dst = mixed[:, place(c), :] if c < gates else scaled[0:rows, place(c), :]
                    dve.tensor_tensor(dst, ps_h[0:rows, NW * bank(b, c) + 1, :], hidden[0:rows, place(c), :], ALU.mult).then_inc(mixed_done, 1)
                    if c > 0:
                        dve.wait_ge(mixed_done, b.counted(chunks, c))
                        dve.wait_ge(spread, b.counted(gates, c))
                        dve.tensor_tensor(scaled[:, place(c - 1), :], mixed[:, place(c - 1), :], ps_gate[:, 0, :], ALU.mult).then_inc(scaled_done, 1)
                else:
                    g = c // per_gate
                    dve.wait_ge(spread, b.counted(gates, g + 1))
                    dve.tensor_tensor(scaled[:, place(c), :], hidden[:, place(c), :], ps_gate[:, g % GR, :], ALU.mult).then_inc(scaled_done, 1)

            def step(t):
                new, cur, old = t, t.back(1), t.back(2)
                links = Links(new, CHAIN)
                for s in range(chunks):
                    if cur.there():
                        scale(cur, s)
                    if norm_in and s == slots["stats"] and new.there():
                        dve.wait_ge(x_loaded[new.r], new.used(16))
                        norm_stats(new, x_in[:, new.r], 0, in_stats, in_aggr, in_eps, in_normed)
                    if norm_in and s == slots["norm"] and new.there():
                        if positive(count := new.counted(1, 0)):
                            dve.wait_ge(xt_done, count)
                        norm_apply(new, x_in[:, new.r], x_norm, 0, in_rstd, in_normed)
                    if s == slots["turn_x"] + 1 and new.there():
                        dve.wait_ge(hi_ready, new.counted(1, 1))
                        if positive(count := new.counted(chunks, (1 - BRING) * chunks)):
                            dve.wait_ge(first_done, count)
                        dve.tensor_tensor(x_lo[:, new.r], ps_turn[:], x_hi[:, new.r].bitcast(F32), ALU.subtract).then_inc(lo_ready, 1)
                    if s == slots["route"] + 1 and new.there():
                        route_first(new, links)
                    if gated and s == slots["score"] + 1 and new.there():
                        route_groups(new, links)
                    if gated and s == slots["score"] + 2 and new.there():
                        route_mask(links)
                    if gated and slots["rank"] <= s < slots["rank"] + 5 and new.there():
                        rank_of(logits[:], E, BT, rank[:], links, [s - slots["rank"]])
                    if s == slots["weigh"] and new.there():
                        route_weights(new, links)
                    for n in range(len(pieces)):
                        if s == slots["split"][n] and new.i is None and new.c == 0:
                            dve.wait_ge(raw_hi, n + 1)
                            dve.tensor_tensor(piece_of(w_lo, n), piece_of(w_raw, n), piece_of(w_hi, n).bitcast(F32), ALU.subtract).then_inc(raw_split, 1)
                    if s == slots["turn_y"] + 1 and old.there():
                        dve.wait_ge(y_turned, old.counted(1, 1))
                        if norm_in:
                            dve.wait_ge(res_ready, old.counted(1, 1))
                        else:
                            dve.wait_ge(res_loaded[old.r], old.used(16))
                        if positive(count := old.counted(BT, 0)):
                            dve.wait_ge(y_done, count)
                        dve.tensor_tensor(y_sum[:], ps_turn.rearrange("p (t d) -> p t d", t=BT), x_res[:, 0, old.r], ALU.add).then_inc(summed, 1)
                        dve.wait_ge(summed, old.counted(1, 1))
                        norm_stats(old, y_sum, 1, out_stats, out_aggr, out_eps, y_done)
                    if s == slots["norm_y"] and old.there():
                        if old.i is not None or old.c >= BRING:
                            dve.wait_ge(stored[old.r], old.back(BRING).used(16))
                        norm_apply(old, y_sum, y_out[:, old.r], 1, out_rstd, y_done)

            run_turns(dve, step, first, NB, NB + 2, BRING)


def stack_selection(hd):
    parts = 1 if hd == 4 else 2
    sel = np.zeros((P, 2, parts, NG, P), np.float32)
    for which, slots in enumerate(((0, 0, 1), (0, 1, 0))):
        for h in range(H):
            g = h % GH
            for slot, part in enumerate(slots):
                for d in range(hd):
                    src = h * hd + d + (part * H * hd if parts == 1 else 0)
                    sel[src, which, part if parts == 2 else 0, h // GH, ROWS * g + slot * hd + d] = 1
    return sel.reshape(P, -1)


def columns(hd, bias_q=None, bias_k=None):
    col = np.zeros((P, 8), np.float32)
    if bias_q is not None:
        col[:, 0], col[:, 1] = bias_q, bias_k
    for g in range(GH):
        col[ROWS * g + 3 * hd:ROWS * g + 3 * hd + 2, 2] = 1
    col[P // 2:, 3] = -1
    return col


def attention_layout(hd, q_t, k_t, v_t, o_t, bias_q=None, bias_k=None, bias_v=None, bias_o=None, norm_w=None, norm_b=None):
    HD = H * hd
    qk = np.zeros((P, 2, P), np.float32)
    for which, wt in enumerate((q_t, k_t)):
        for copy in range(P // HD):
            qk[0:wt.shape[0], which, copy * HD:(copy + 1) * HD] = wt
    v = np.zeros((P, HD), np.float32)
    v[0:v_t.shape[0]] = v_t
    rows = np.zeros((1, 2, D), np.float32)
    rows[0, 1] = 1
    if bias_v is not None:
        rows[0, 0] = bias_v
    wide = np.zeros((P, 3, D), np.float32)
    for n, row in enumerate((bias_o, norm_w, norm_b)):
        if row is not None:
            wide[:, n, :] = row[None, :]
    masks = np.zeros((P, 2, P), np.float32)
    masks[:, 0][np.triu_indices(P, 1)] = MASKED
    masks[:, 1][np.tril_indices(P, -1)] = MASKED
    return {"qk": qk, "v": v, "o": np.ascontiguousarray(o_t), "sel": stack_selection(hd), "col": columns(hd, bias_q, bias_k),
            "rows": rows, "wide": wide, "ident": np.eye(P, dtype=np.float32), "masks": masks}


def expert_layout(first_t, second_t, gate_t, gate_bias=None, b_hidden=None, b_out=None, norm_w=None, norm_b=None):
    E = gate_t.shape[1]
    units = first_t[0].shape[1]
    chunks = -(-units // P)
    gated = len(first_t) == 2
    first = np.zeros((P, chunks, len(first_t), P), np.float32)
    for k, wt in enumerate(first_t):
        for c in range(chunks):
            n = min(P, units - c * P)
            first[:, c, k, 0:n] = wt[:, c * P:c * P + n]
    second = np.zeros((P, chunks, D), np.float32)
    for c in range(chunks):
        n = min(P, units - c * P)
        second[0:n, c, :] = second_t[c * P:c * P + n]
    gates = chunks - 1 if gated else E
    sel = np.zeros((P, gates, P), np.float32)
    for g in range(gates):
        for j in range(P):
            e = (g * P + j) * E // (gates * P) if gated else g
            sel[e, g, j] = sel[LO + e, g, j] = 1
    wide = np.zeros((P, 2, D), np.float32)
    for n, row in enumerate((norm_w, norm_b)):
        if row is not None:
            wide[:, n, :] = row[None, :]
    out = {"first": first, "second": second, "gate": np.ascontiguousarray(gate_t), "wide": wide, "sel": sel,
           "ident": np.eye(P, dtype=np.float32), "before": np.broadcast_to(np.tri(E, k=-1, dtype=np.float32), (P, E, E)).copy(),
           "gate_bias": np.zeros((P, E), np.float32), "b_hidden": np.zeros((P, chunks), np.float32), "b_out": np.zeros((P, D), np.float32)}
    if gate_bias is not None:
        out["gate_bias"][:] = gate_bias[None, :]
    if b_hidden is not None:
        out["b_hidden"][:] = b_hidden.reshape(chunks, P).T
    if b_out is not None:
        out["b_out"][0:E] = b_out
        out["b_out"][LO:LO + E] = b_out
    return out


def two_layers(nc, x, y, stage_inputs):
    between = [nc.dram_tensor(f"after_stage_{n}", (B, S, D), F32, kind="Internal").ap() for n in range(4)]
    a, b, e1, c, e2 = stage_inputs
    with nc.sbuf_tensor("k_blocks", [P, RING, NG, GH, S], F32R) as k_blocks:
        attention_stage(nc, "a", k_blocks, hd=4, causal=False, norm_in=False, norm_out=True, clear_blocks=True, x=x, y=between[0], w=a)
        attention_stage(nc, "b", k_blocks, hd=8, causal=True, norm_in=True, norm_out=False, clear_blocks=False, x=between[0], y=between[1], w=b)
        expert_stage(nc, "e1", experts=8, chunks=32, last_rows=P, gated=False, slots=SLOTS_1, x=between[1], x_more=between[0], y=between[2], w=e1)
        attention_stage(nc, "c", k_blocks, hd=8, causal=True, norm_in=False, norm_out=True, clear_blocks=False, x=between[2], y=between[3], w=c)
        expert_stage(nc, "e2", experts=16, chunks=13, last_rows=96, gated=True, slots=SLOTS_2, x=between[3], x_more=None, y=y, w=e2)


def layouts(i):
    qkv_b, bias_b = i["L0_ffn_Wqkv"], i["L0_ffn_bqkv"]
    qkv_c, bias_c = i["L1_attn_W_qkv"].T, i["L1_attn_b_qkv"]
    q, k, v = slice(0, D), slice(D, 2 * D), slice(2 * D, 3 * D)

    def units(w):
        return w.transpose(0, 2, 1).reshape(-1, D)

    a = attention_layout(4, i["L0_attn_Wq"].T, i["L0_attn_Wk"].T, i["L0_attn_Wv"].T, i["L0_attn_Wo"].T, bias_o=i["L0_attn_bo"])
    b = attention_layout(8, qkv_b[:, q], qkv_b[:, k], qkv_b[:, v], i["L0_ffn_Wo"], bias_b[q], bias_b[k], bias_b[v], i["L0_ffn_bo"],
                         i["L0_ffn_ln1_w"], i["L0_ffn_ln1_b"])
    e1 = expert_layout([i["L0_ffn_fc1_w"].reshape(-1, D).T], units(i["L0_ffn_fc2_w"]), i["L0_ffn_gate_W"],
                       b_hidden=i["L0_ffn_fc1_b"].reshape(-1), b_out=i["L0_ffn_fc2_b"], norm_w=i["L0_ffn_ln2_w"], norm_b=i["L0_ffn_ln2_b"])
    c = attention_layout(8, qkv_c[:, q], qkv_c[:, k], qkv_c[:, v], i["L1_attn_W_o"].T, bias_c[q], bias_c[k], bias_c[v], i["L1_attn_b_o"])
    gate = np.concatenate([i["L1_ffn_w1"].reshape(-1, D), i["L1_ffn_ws1"]]).T
    up = np.concatenate([i["L1_ffn_w3"].reshape(-1, D), i["L1_ffn_ws3"]]).T
    down = np.concatenate([units(i["L1_ffn_w2"]), i["L1_ffn_ws2"].T])
    e2 = expert_layout([gate, up], down, i["L1_ffn_gate_w"].T, gate_bias=i["L1_ffn_gate_bias"])
    return {"a": a, "b": b, "e1": e1, "c": c, "e2": e2}


def kernel(**inputs):
    import concourse.bacc as bacc
    from concourse.bass_utils import run_bass_kernel_spmd

    nc = bacc.Bacc("TRN2", target_bir_lowering=False, num_devices=1)
    arrays = {name: np.asarray(value) for name, value in inputs.items()}
    fed = {"x": np.ascontiguousarray(arrays["L0_attn_x"])}
    x = nc.dram_tensor("x", (B, S, D), F32, kind="ExternalInput").ap()
    y = nc.dram_tensor("y", (B, S, D), F32, kind="ExternalOutput").ap()
    stage_inputs = []
    for stage, laid in layouts(arrays).items():
        aps = {}
        for name, a in laid.items():
            fed[f"in_{stage}_{name}"] = np.ascontiguousarray(a)
            aps[name] = nc.dram_tensor(f"in_{stage}_{name}", a.shape, F32, kind="ExternalInput").ap()
        stage_inputs.append(aps)
    two_layers(nc, x, y, stage_inputs)
    result = run_bass_kernel_spmd(nc, [fed], core_ids=[0])
    return result.results[0]["y"]
```

```python
from contextlib import ExitStack

import numpy as np

import concourse.bass as bass
from concourse import mybir

F32 = mybir.dt.float32
F32R = mybir.dt.float32r
BF16 = mybir.dt.bfloat16
ALU = mybir.AluOpType
ACT = mybir.ActivationFunctionType
AX = mybir.AxisListType

P = 128
B, S, D = 16, 256, 128
H = 16
NT = S // P
ROWS = 32
NG = H * ROWS // P
GH = P // ROWS
EPS = 1e-5
MASKED = -1e30
SCALE = float(D // H) ** -0.5
RING = 3


class Turn:

    def __init__(self, i, c, total, ring):
        self.i, self.c, self.total, self.ring = i, c, total, ring
        self.r = c % ring

    def back(self, n):
        return Turn(self.i, self.c - n, self.total, self.ring)

    def there(self):
        return self.i is not None or 0 <= self.c < self.total

    def counted(self, per, more=0):
        fixed = self.c * per + more
        return min(fixed, self.total * per) if self.i is None else self.i * (self.ring * per) + fixed

    def used(self, per):
        fixed = (self.c // self.ring + 1) * per
        return fixed if self.i is None else self.i * per + fixed

    def of(self, view):
        if self.i is None:
            return view[self.c]
        return view[bass.ds(self.i * self.ring + self.c, 1)].rearrange("a p t d -> p (a t) d")


def positive(count):
    return not isinstance(count, int) or count > 0


def run_turns(eng, step, first, batches, turns, ring=RING):
    for t in range(first):
        step(Turn(None, t, batches, ring))
    rounds = (batches - first) // ring
    with eng.Fori(0, rounds) as i:
        for u in range(ring):
            step(Turn(i, first + u, batches, ring))
    for t in range(first + rounds * ring, turns):
        step(Turn(None, t, batches, ring))


def stage_semaphores(nc, ctx, tag):
    taken = []

    def sem(name):
        taken.append(nc.alloc_semaphore(f"{tag}_{name}"))
        return taken[-1]

    def clear():
        nc.clear_and_free_semaphores(taken)
        nc.all_engine_barrier()

    ctx.callback(clear)
    return sem


class Memory:

    def __init__(self, nc, ctx, tag, k_blocks):
        def sb(name, shape, dt=F32):
            return ctx.enter_context(nc.sbuf_tensor(f"{tag}_{name}", shape, dt))

        self.k_blocks = k_blocks
        self.k_stack = sb("k_stack", [P, NG, S], F32R)
        self.q_stack = sb("q_stack", [P, RING, NG, S], F32R)
        self.q_shift = sb("q_shift", [P, RING, NG, S], F32R)
        self.v_ones = sb("v_ones", [P, RING, NT, H, ROWS])
        self.probs = sb("probs", [P, 2 * GH, 2 * S])
        self.out_t = sb("out_t", [P, NG, S])
        self.neg_max = sb("neg_max", [P, NT, H])
        self.max_rows = sb("max_rows", [P, NT, H, ROWS])
        self.x_in = sb("x_in", [P, RING, NT, D])
        self.x_res = sb("x_res", [P, RING, NT, D])
        self.x_norm = sb("x_norm", [P, RING, NT, D])
        self.x_t = sb("x_t", [P, S])
        self.qk_hi = sb("qk_hi", [P, 2, S], F32R)
        self.qk_lo = sb("qk_lo", [P, 2, S], F32R)
        self.inv_sum = sb("inv_sum", [P, NT, H])
        self.out_n = sb("out_n", [P, NT, D])
        self.out_nt = sb("out_nt", [P, S])
        self.y = sb("y_sum", [P, NT, D])
        self.y_out = sb("y_out", [P, RING, NT, D])
        self.stats = sb("stats", [P, NT, 6])
        self.mean_var = sb("mean_var", [P, NT + 1, 2])
        self.var_eps = sb("var_eps", [P, NT])
        self.rstd = sb("rstd", [P, NT])
        self.stats_in = sb("stats_in", [P, NT, 6])
        self.mean_var_in = sb("mean_var_in", [P, NT + 1, 2])
        self.var_eps_in = sb("var_eps_in", [P, NT])
        self.rstd_in = sb("rstd_in", [P, NT])
        self.w_qk = sb("w_qk", [P, 2, P])
        self.w_v = sb("w_v", [P, D])
        self.w_o = sb("w_o", [P, D])
        self.sel = sb("sel", [P, 2, 2, NG, P], F32R)
        self.col = sb("col", [P, 8])
        self.wide = sb("wide", [P, 4, D])
        self.carry = sb("carry", [P, NT])
        self.ident = sb("ident", [P, P])
        self.ident_bf = sb("ident_bf", [P, P], BF16)
        self.mask_f32 = sb("mask_f32", [P, P])
        self.mask = sb("mask", [P, GH, P], BF16)
        self.neg_half = sb("neg_half", [P, NT])


SLOTS = {
    "weigh": (9, 13, 2, 5),
    "turn_max": 0, "turn_x": 2, "project_qk": 4, "turn_out": 7, "project_v": 6, "stack_k": 9, "turn_norm": 11, "stack_q": 12, "project_out": 14,
    "copy_x": 2, "copy_hi": 4, "copy_out_1": 5, "copy_v": 6, "copy_k": 9, "copy_norm": 11, "copy_q": 12, "copy_out_0": 13,
    "shift": 0, "split_lo": 5, "divide": 7, "in_stats": 8, "in_norm": 11, "add_out": 14, "norm_out": 15,
    "add_bias": 2}
SLOTS_NORM = {**SLOTS, "turn_norm": 10, "copy_norm": 10, "project_out": 12, "add_out": 13, "stack_q": 13, "copy_q": 13,
              "turn_out": 6, "divide": 6, "stack_k": 8, "copy_k": 8,
              "project_v": 7, "copy_v": 7}
SLOTS_FULL = {**SLOTS_NORM, "turn_max": 1, "shift": 1, "turn_x": 1, "copy_x": 1}


def attention_stage(nc, tag, k_blocks, hd, causal, norm_in, norm_out, clear_blocks, x, y, w):
    row_hi, row_lo = 3 * hd, 3 * hd + 1
    HD = H * hd
    parts = 1 if hd == 4 else 2
    x_v = x.rearrange("b (t p) d -> b p t d", p=P)
    y_v = y.rearrange("b (t p) d -> b p t d", p=P)
    lag = 1 if norm_in else 0
    total = B + 3 + lag
    first = 7
    at = SLOTS_FULL if not causal else SLOTS_NORM if norm_out else SLOTS
    if causal:
        max_ops = [(0, slice(0, GH), slice(0, P)), (1, slice(0, 2), slice(0, S)), (1, slice(2, 4), slice(0, S))]
    else:
        max_ops = [(qt, slice(2 * j, 2 * j + 2), slice(0, S)) for qt in range(NT) for j in range(2)]
    KM = NG * len(max_ops)
    MAX_FROM = (H - KM) // 2
    CLEARED = 3 if clear_blocks else 2
    EW = S + P if causal else 2 * S

    with ExitStack() as ctx:
        m = Memory(nc, ctx, tag, k_blocks)

        sem = stage_semaphores(nc, ctx, tag)

        def psum(name, shape):
            return ctx.enter_context(nc.psum_tensor(f"{tag}_{name}", shape, F32))

        ps_max = psum("ps_max", [P, 2, 2 * S])
        ps_exp = psum("ps_exp", [P, 2, 2 * S])
        ps_out = psum("ps_out", [P, 2, S])
        ps_wide = psum("ps_wide", [P, NG, S])
        ps_small = psum("ps_small", [P, 2, S])

        sel_loaded = sem("sel_loaded")
        loaded_first = sem("loaded_first")
        loaded = sem("loaded")
        const_ready = sem("const_ready")
        cleared = sem("cleared")
        x_loaded = [sem(f"x_loaded{r}") for r in range(RING)]
        res_loaded = [sem(f"res_loaded{r}") for r in range(RING)]
        stored = [sem(f"stored{r}") for r in range(RING)]
        blocks_loaded = [sem(f"blocks_loaded{r}") for r in range(RING)]
        xt_done, qk_done, v_done = sem("xt_done"), sem("qk_done"), sem("v_done")
        k_stacked, q_stacked = sem("k_stacked"), sem("q_stacked")
        max_scored, max_turned = sem("max_scored"), sem("max_turned")
        exp_scored, weighed = sem("exp_scored"), sem("weighed")
        out_turned, norm_turned, projected = sem("out_turned"), sem("norm_turned"), sem("projected")
        xt_copied, hi_ready, v_copied = sem("xt_copied"), sem("hi_ready"), sem("v_copied")
        k_copied, q_copied = sem("k_copied"), sem("q_copied")
        exp_done, out_copied, norm_copied = sem("exp_done"), sem("out_copied"), sem("norm_copied")
        lo_ready, max_done, max_hi, rows_ready = sem("lo_ready"), sem("max_done"), sem("max_hi"), sem("rows_ready")
        shifted, inv_done, divided, summed = sem("shifted"), sem("inv_done"), sem("divided"), sem("summed")
        stats_done, aggr_done, eps_done, y_done = sem("stats_done"), sem("aggr_done"), sem("eps_done"), sem("y_done")
        v_cleared = sem("v_cleared")
        in_stats, in_aggr, in_eps, in_normed = sem("in_stats"), sem("in_aggr"), sem("in_eps"), sem("in_normed")
        bias_added, rstd_done, masked = sem("bias_added"), sem("rstd_done"), sem("masked")
        in_rstd, in_scaled, in_ready = sem("in_rstd"), sem("in_scaled"), sem("in_ready")

        later = [(m.w_v[:, 0:HD], w["v"]), (m.wide[:], w["wide"]), (m.mask_f32[:], w["mask"]), (m.w_o[0:HD, :], w["o"])]
        LOADED = 16 * len(later)

        block = ctx.enter_context(nc.Block())

        @block.sync
        def _(sp):
            for dst, src in ((m.ident[:], w["ident"]), (m.w_qk[:], w["qk"]), (m.col[:], w["col"])):
                sp.dma_start(dst, src).then_inc(loaded_first, 16)

            def step(t):
                if t.there():
                    if positive(count := t.counted(NT if norm_in else 1, (1 - RING) * (NT if norm_in else 1))):
                        sp.wait_ge(in_normed if norm_in else xt_done, count)
                    sp.dma_start(m.x_in[:, t.r], t.of(x_v)).then_inc(x_loaded[t.r], 16)
                b = t.back(4 + lag)
                if b.there():
                    if positive(count := b.counted(1, 1 - RING)):
                        sp.wait_ge(summed, count)
                    sp.dma_start(m.x_res[:, b.r], b.of(x_v)).then_inc(res_loaded[b.r], 16)
                b = t.back(1 + lag)
                if b.there():
                    sp.wait_ge(loaded_first, 16 * 3)
                    sp.wait_ge(k_copied, b.counted(1, 1))
                    if positive(count := b.counted(H, (1 - RING) * H)):
                        sp.wait_ge(exp_scored, count)
                    if b.i is None and b.c == 0:
                        sp.wait_ge(cleared, CLEARED)
                    for g in range(GH):
                        q = slice(ROWS * g, ROWS * g + ROWS)
                        sp.dma_start(m.k_blocks[q, b.r, :, g, :].bitcast(F32), m.k_stack[q].bitcast(F32)).then_inc(blocks_loaded[b.r], 16)
                b = t.back(5 + lag)
                if b.there():
                    sp.wait_ge(y_done if norm_out else summed, b.counted(NT, NT) if norm_out else b.counted(1, 1))
                    sp.dma_start(b.of(y_v), m.y_out[:, b.r]).then_inc(stored[b.r], 16)

            run_turns(sp, step, first, B, B + 5 + lag)
            for r in range(RING):
                sp.wait_ge(stored[r], 16 * len(range(r, B, RING)))

        @block.gpsimd
        def _(pool):
            pool.dma_start(m.sel[:, :, 0:parts].rearrange("p w a g c -> p w (a g c)"), w["sel"].rearrange("p (w c) -> p w c", w=2).bitcast(F32R)).then_inc(sel_loaded, 16)
            v_flat = m.v_ones.rearrange("p r t h c -> p (r t h) c")
            pool.memset(v_flat, 0.0).then_inc(v_cleared, 1)
            pool.wait_ge(v_cleared, 1)
            pool.memset(v_flat[:, :, hd:hd + 1], 1.0).then_inc(v_cleared, 1)
            pool.memset(m.max_rows[:], 0.0).then_inc(cleared, 1)
            pool.memset(m.neg_half[:], -0.5).then_inc(cleared, 1)
            if clear_blocks:
                pool.memset(m.k_blocks[:].bitcast(F32), 0.0).then_inc(cleared, 1)
            pool.wait_ge(cleared, CLEARED)
            pool.wait_ge(loaded, LOADED)

            def mask_heads(b, h):
                pool.wait_ge(exp_done, b.counted(H, h + 2))
                if positive(count := b.counted(H // 2, h // 2)):
                    pool.wait_ge(masked, count)
                pool.tensor_tensor(m.carry[:], m.neg_half[:], m.neg_half[:], ALU.add)
                place = h % (2 * GH)
                blocks = m.probs[:, place:place + 2, :].rearrange("p h (k q) -> p h k q", k=2)[:, :, :, 0:P]
                pool.affine_select(blocks, blocks, pattern=[[0, 2], [0, 2], [1, P]], compare_op=ALU.is_ge, fill=0.0, base=0,
                                   channel_multiplier=-1).then_inc(masked, 1)

            def step(t):
                ex, tail = t.back(2 + lag), t.back(3 + lag)
                for s in range(H):
                    if causal and s % 2 == 1 and s < 4 and tail.there():
                        mask_heads(tail, 12 + s - 1)
                    if causal and s % 2 == 1 and s >= 4 and ex.there():
                        mask_heads(ex, s - 5)
                    if norm_in and s == at["in_stats"] and t.there():
                        pool.wait_ge(in_eps, t.counted(1, 1))
                        pool.tensor_tensor(m.rstd_in[:], m.var_eps_in[:], m.neg_half[:], ALU.pow).then_inc(in_rstd, 1)
                    if norm_in and s == at["in_norm"] and t.there():
                        pool.wait_ge(in_normed, t.counted(NT, NT))
                        xn = m.x_norm[:, t.r]
                        pool.tensor_tensor(xn, xn, m.wide[:, 1:2, :].to_broadcast([P, NT, D]), ALU.mult).then_inc(in_scaled, 1)
                        pool.wait_ge(in_scaled, t.counted(1, 1))
                        pool.tensor_tensor(xn, xn, m.wide[:, 2:3, :].to_broadcast([P, NT, D]), ALU.add).then_inc(in_ready, 1)
                    if s == at["add_bias"] and tail.there():
                        res = m.x_res[:, tail.r]
                        pool.wait_ge(res_loaded[tail.r], tail.used(16))
                        pool.tensor_tensor(res, res, m.wide[:, 0:1, :].to_broadcast([P, NT, D]), ALU.add).then_inc(bias_added, 1)
                    if norm_out and s == at["add_out"] and tail.there():
                        pool.wait_ge(eps_done, tail.counted(1, 1))
                        pool.tensor_tensor(m.rstd[:], m.var_eps[:], m.neg_half[:], ALU.pow).then_inc(rstd_done, 1)

            run_turns(pool, step, first, B, total)

        @block.tensor
        def _(pe):
            def weigh(b, group):
                if causal:
                    pe.wait_ge(masked, b.counted(H // 2, (GH * group + GH) // 2))
                else:
                    pe.wait_ge(exp_done, b.counted(H, GH * group + GH))
                if group == 0:
                    pe.wait_ge(v_copied, b.counted(1, 1))
                if group % 2 == 0:
                    if positive(count := b.counted(2, group // 2)):
                        pe.wait_ge(out_copied, count)
                for kt in range(NT):
                    for g in range(GH):
                        h = GH * group + g
                        lhs = m.v_ones[:, b.r, kt, h, :]
                        if causal and kt == 1:
                            rhs, q0 = m.probs[:, h % (2 * GH), S:S + P], P
                        else:
                            rhs, q0 = m.probs[:, h % (2 * GH), kt * S:kt * S + S], 0
                        ins = pe.matmul(ps_out[ROWS * g:ROWS * g + ROWS, group % 2, q0:S], lhs, rhs, start=(kt == 0), stop=(kt == NT - 1))
                ins.then_inc(weighed, 1)

            def score_for_exp(b, h):
                if h == 0:
                    pe.wait_ge(shifted, b.counted(1, 1))
                n = b.counted(H, h - 1)
                if positive(count := n):
                    pe.wait_ge(exp_done, count)
                G, g = divmod(h, GH)
                bank = ps_exp[:, h % 2, :]
                for kt in range(NT):
                    keys = m.k_blocks[:, b.r, G, g, kt * P:kt * P + P]
                    if causal and kt == 1:
                        ins = pe.matmul(bank[:, S:S + P], keys, m.q_shift[:, b.r, G, P:S], start=False, stop=True, skip_group_check=True)
                    else:
                        ins = pe.matmul(bank[:, kt * S:kt * S + S], keys, m.q_shift[:, b.r, G, :], start=(kt == 0), stop=True, skip_group_check=True)
                ins.then_inc(exp_scored, 1)

            def score_for_max(b, n):
                G, o = divmod(n, len(max_ops))
                qt, heads, keys = max_ops[o]
                if n == 0:
                    pe.wait_ge(q_copied, b.counted(1, 1))
                    pe.wait_ge(blocks_loaded[b.r], b.used(16 * GH))
                if positive(count := b.counted(KM, n - 1)):
                    pe.wait_ge(max_done, count)
                queries = m.q_stack[:, b.r, G, qt * P:qt * P + P]
                bank = ps_max[:, n % 2, :]
                ins = pe.matmul(bank, queries, m.k_blocks[:, b.r, G, heads, keys], start=True, stop=not causal, skip_group_check=True)
                if causal and qt == 0:
                    ins = pe.matmul(bank, m.ident_bf[:], m.mask[:], start=False, stop=True, skip_group_check=True)
                if causal and qt == 1:
                    out = bank.rearrange("p (h k) -> p h k", h=2)[:, :, P:S]
                    ins = pe.matmul(out, m.ident_bf[:], m.mask[:, 0:2, :], start=False, stop=True, skip_group_check=True)
                ins.then_inc(max_scored, 1)

            def turn_max(b):
                pe.wait_ge(rows_ready, b.counted(1, 1))
                if positive(count := b.counted(1, -1)):
                    pe.wait_ge(divided, count)
                pe.wait_ge(q_copied, b.counted(1, 2))
                for G in range(NG):
                    for qt in range(NT):
                        ins = pe.transpose(ps_wide[:, G, qt * P:qt * P + P], m.max_rows[:, qt, GH * G:GH * G + GH, :], m.ident[:])
                ins.then_inc(max_turned, 1)

            def stack(b, which, done):
                for G in range(NG):
                    for part in range(parts):
                        src = (m.qk_hi, m.qk_lo)[part] if parts == 2 else m.qk_lo
                        ins = pe.matmul(ps_wide[:, G, :], m.sel[:, which, part, G, :], src[:, which, :], start=(part == 0), stop=(part == parts - 1),
                                        skip_group_check=True)
                ins.then_inc(done, 1)

            def step(t):
                prep, mx, ex, tail = t.back(lag), t.back(1 + lag), t.back(2 + lag), t.back(3 + lag)
                if mx.i is None and mx.c == 0:
                    pe.wait_ge(const_ready, 2 + (HD < D))
                for s in range(H):
                    if s == at["project_v"] and prep.i is None and prep.c == 0:
                        pe.wait_ge(loaded, LOADED)
                        pe.wait_ge(sel_loaded, 16)
                    if mx.there() and 0 <= s - MAX_FROM < KM:
                        score_for_max(mx, s - MAX_FROM)
                    if s == at["turn_max"] and ex.there():
                        turn_max(ex)
                    if s < 4 and tail.there():
                        score_for_exp(tail, 12 + s)
                    if s >= 4 and ex.there():
                        score_for_exp(ex, s - 4)
                    if s == at["weigh"][2] and tail.there():
                        weigh(tail, 2)
                    if s == at["weigh"][3] and tail.there():
                        weigh(tail, 3)
                    if s == at["weigh"][0] and ex.there():
                        weigh(ex, 0)
                    if s == at["weigh"][1] and ex.there():
                        weigh(ex, 1)
                    if s == at["turn_x"] and prep.there():
                        if norm_in:
                            pe.wait_ge(in_ready, prep.counted(1, 1))
                        else:
                            pe.wait_ge(x_loaded[prep.r], prep.used(16))
                        if positive(count := prep.counted(1, -3)):
                            pe.wait_ge(summed, count)
                        if positive(count := prep.counted(1, 0)):
                            pe.wait_ge(v_copied, count)
                        src = m.x_norm if norm_in else m.x_in
                        for tile in range(NT):
                            ins = pe.transpose(ps_small[:, 0, tile * P:tile * P + P], src[:, prep.r, tile, :], m.ident[:])
                        ins.then_inc(xt_done, 1)
                    if s == at["project_qk"] and prep.there():
                        pe.wait_ge(xt_copied, prep.counted(1, 1))
                        for which in range(2):
                            ins = pe.matmul(ps_small[:, which, :], m.w_qk[:, which, :], m.x_t[:], start=True, stop=True)
                        ins.then_inc(qk_done, 1)
                    if s == at["project_v"] and prep.there():
                        pe.wait_ge(lo_ready, prep.counted(1, 1))
                        for tile in range(NT):
                            out = ps_small[:, 0, tile * HD:tile * HD + HD]
                            ins = pe.matmul(out, m.x_t[:, tile * P:tile * P + P], m.w_v[:, 0:HD], start=True, stop=True)
                        ins.then_inc(v_done, 1)
                    if s == at["turn_out"] and tail.there():
                        pe.wait_ge(out_copied, tail.counted(2, 2))
                        pe.wait_ge(shifted, tail.counted(1, 2))
                        for G in range(NG):
                            for qt in range(NT):
                                ins = pe.transpose(ps_wide.rearrange("p g s -> p (g s)")[:, (qt * NG + G) * P:(qt * NG + G + 1) * P],
                                                   m.out_t[:, G, qt * P:qt * P + P], m.ident[:])
                        ins.then_inc(out_turned, 1)
                    if s == at["stack_k"] and prep.there():
                        pe.wait_ge(lo_ready, prep.counted(1, 1))
                        if positive(count := prep.counted(1, -2)):
                            pe.wait_ge(divided, count)
                        stack(prep, 1, k_stacked)
                    if s == at["stack_q"] and prep.there():
                        pe.wait_ge(k_copied, prep.counted(1, 1))
                        stack(prep, 0, q_stacked)
                    if s == at["turn_norm"] and tail.there():
                        pe.wait_ge(divided, tail.counted(1, 1))
                        pe.wait_ge(v_copied, tail.counted(1, 4))
                        for qt in range(NT):
                            ins = pe.transpose(ps_small[:, 1, qt * P:qt * P + P], m.out_n[:, qt, :], m.ident[:])
                        ins.then_inc(norm_turned, 1)
                    if s == at["project_out"] and tail.there():
                        pe.wait_ge(norm_copied, tail.counted(1, 1))
                        for qt in range(NT):
                            ins = pe.matmul(ps_small[:, 0, qt * D:qt * D + D], m.out_nt[0:HD, qt * P:qt * P + P], m.w_o[0:HD, :], start=True, stop=True)
                        ins.then_inc(projected, 1)

            pe.wait_ge(loaded_first, 16 * 3)
            run_turns(pe, step, first, B, total)

        @block.scalar
        def _(act):
            def exp(b, h):
                act.wait_ge(exp_scored, b.counted(H, h + 1))
                if positive(count := b.counted(NG, h // GH - 1)):
                    act.wait_ge(weighed, count)
                act.activation(m.probs[:, h % (2 * GH), 0:EW], exp_cols(h), ACT.Exp, scale=SCALE).then_inc(exp_done, 1)

            def exp_cols(h):
                return ps_exp[:, h % 2, 0:EW]

            def copy_out(b, half):
                act.wait_ge(weighed, b.counted(NG, 2 * half + 2))
                if half == 0:
                    if positive(count := b.counted(1, 0)):
                        act.wait_ge(out_turned, count)
                act.activation(m.out_t[:, 2 * half:2 * half + 2, :], ps_out[:], ACT.Copy).then_inc(out_copied, 1)

            def step(t):
                prep, ex, tail = t.back(lag), t.back(2 + lag), t.back(3 + lag)
                for s in range(H):
                    if s < 4 and tail.there():
                        exp(tail, 12 + s)
                    if s >= 4 and ex.there():
                        exp(ex, s - 4)
                    if s == at["copy_x"] and prep.there():
                        act.wait_ge(xt_done, prep.counted(1, 1))
                        if positive(count := prep.counted(1, 0)):
                            act.wait_ge(v_done, count)
                        act.activation(m.x_t[:], ps_small[:, 0, :], ACT.Copy).then_inc(xt_copied, 1)
                    if s == at["copy_hi"] and prep.there():
                        act.wait_ge(qk_done, prep.counted(1, 1))
                        if positive(count := prep.counted(1, 0)):
                            act.wait_ge(q_stacked, count)
                        for which in range(2):
                            act.activation(m.qk_hi[:, which, :], ps_small[:, which, :], ACT.Identity, bias=m.col[:, which:which + 1]).then_inc(hi_ready, 1)
                    if s == at["copy_out_1"] and tail.there():
                        copy_out(tail, 1)
                    if hd == 4 and s == at["copy_v"] and prep.there():
                        act.wait_ge(v_done, prep.counted(1, 1))
                        if positive(count := prep.counted(NG, (1 - RING) * NG)):
                            act.wait_ge(weighed, count)
                        src = ps_small[:, 0, 0:NT * HD].rearrange("p (t h d) -> p t h d", t=NT, h=H)
                        act.activation(m.v_ones[:, prep.r, :, :, 0:hd], src, ACT.Copy).then_inc(v_copied, 1)
                    if s == at["copy_k"] and prep.there():
                        act.wait_ge(k_stacked, prep.counted(1, 1))
                        if prep.i is not None or prep.c > 0:
                            p = prep.back(1)
                            act.wait_ge(blocks_loaded[p.r], p.used(16 * GH))
                        act.activation(m.k_stack[:], ps_wide[:], ACT.Identity, bias=m.col[:, 2:3]).then_inc(k_copied, 1)
                    if s == at["copy_q"] and prep.there():
                        act.wait_ge(q_stacked, prep.counted(1, 1))
                        if positive(count := prep.counted(1, 1 - RING)):
                            act.wait_ge(shifted, count)
                        act.activation(m.q_stack[:, prep.r], ps_wide[:], ACT.Copy).then_inc(q_copied, 1)
                    if s == at["copy_norm"] and tail.there():
                        act.wait_ge(norm_turned, tail.counted(1, 1))
                        if positive(count := tail.counted(1, 0)):
                            act.wait_ge(projected, count)
                        act.activation(m.out_nt[0:HD, :], ps_small[0:HD, 1, :], ACT.Copy).then_inc(norm_copied, 1)
                    if s == at["copy_out_0"] and ex.there():
                        copy_out(ex, 0)

            for dst, src in later:
                act.dma_start(dst, src).then_inc(loaded, 16)
            act.wait_ge(loaded_first, 16 * 3)
            act.wait_ge(v_cleared, 2)
            run_turns(act, step, first, B, total)

        @block.vector
        def _(dve):
            if HD < D:
                dve.memset(m.out_n[:, :, HD:D], 0.0).then_inc(const_ready, 1)
            dve.wait_ge(loaded_first, 16 * 3)
            dve.tensor_copy(m.ident_bf[:], m.ident[:]).then_inc(const_ready, 1)
            dve.wait_ge(loaded, LOADED)
            dve.tensor_copy(m.mask[:], m.mask_f32[:].unsqueeze(1).to_broadcast([P, GH, P])).then_inc(const_ready, 1)
            dve.wait_ge(cleared, 2)

            def reduce(b, n):
                G, o = divmod(n, len(max_ops))
                qt, heads, keys = max_ops[o]
                nh, nk = heads.stop - heads.start, keys.stop - keys.start
                dve.wait_ge(max_scored, b.counted(KM, n + 1))
                if n == 0:
                    if positive(count := b.counted(1, 0)):
                        dve.wait_ge(rows_ready, count)
                dve.tensor_reduce(m.neg_max[:, qt, GH * G + heads.start:GH * G + heads.stop],
                                  ps_max[:, n % 2, :].rearrange("p (h k) -> p h k", h=nh), AX.X, ALU.max, negate=True).then_inc(max_done, 1)

            def split_max(b):
                dve.wait_ge(max_done, b.counted(KM, KM))
                if positive(count := b.counted(1, 0)):
                    dve.wait_ge(max_turned, count)
                dve.tensor_copy(m.max_rows[:, :, :, row_hi].bitcast(F32R), m.neg_max[:]).then_inc(max_hi, 1)
                dve.wait_ge(max_hi, b.counted(1, 1))
                dve.tensor_tensor(m.max_rows[:, :, :, row_lo].bitcast(F32R), m.neg_max[:], m.max_rows[:, :, :, row_hi], ALU.subtract).then_inc(rows_ready, 1)

            def norm(b, src, dst, stats, mean_var, var_eps, rstd, sems, part):
                s_stats, s_aggr, s_eps, s_rstd, s_done = sems
                if part == 0:
                    if positive(count := b.counted(NT, 0)):
                        dve.wait_ge(s_done, count)
                    for tile in range(NT):
                        dve.bn_stats(stats[:, tile, :], src[:, tile, :]).then_inc(s_stats, 1)
                    dve.wait_ge(s_stats, b.counted(NT, NT))
                    dve.tensor_copy(mean_var[:, NT, 0:1], stats[:, 0, 1:2]).then_inc(s_aggr, 1)
                    for tile in range(NT):
                        dve.bn_aggr(mean_var[:, tile, :], stats[:, tile, :]).then_inc(s_aggr, 1)
                    dve.wait_ge(s_aggr, b.counted(NT + 1, NT + 1))
                    dve.tensor_scalar(var_eps[:], mean_var[:, 0:NT, 1], EPS, None, ALU.add).then_inc(s_eps, 1)
                else:
                    dve.wait_ge(s_rstd, b.counted(1, 1))
                    for tile in range(NT):
                        dve.tensor_scalar(dst[:, tile, :], src[:, tile, :], mean_var[:, tile, 0:1], rstd[:, tile:tile + 1],
                                          ALU.subtract, ALU.mult).then_inc(s_done, 1)

            def step(t):
                prep, mx, ex, tail = t.back(lag), t.back(1 + lag), t.back(2 + lag), t.back(3 + lag)
                for s in range(H):
                    if mx.there() and 0 <= s - MAX_FROM < KM:
                        reduce(mx, s - MAX_FROM)
                    if mx.there() and s == MAX_FROM + KM - 1:
                        split_max(mx)
                    if norm_in and t.there() and s in (at["in_stats"], at["in_norm"]):
                        if s == at["in_stats"]:
                            dve.wait_ge(x_loaded[t.r], t.used(16))
                        else:
                            if positive(count := t.counted(1, 1 - RING)):
                                dve.wait_ge(xt_done, count)
                        norm(t, m.x_in[:, t.r], m.x_norm[:, t.r], m.stats_in, m.mean_var_in, m.var_eps_in, m.rstd_in,
                             (in_stats, in_aggr, in_eps, in_rstd, in_normed), 0 if s == at["in_stats"] else 1)
                    if s == at["shift"] and ex.there():
                        dve.wait_ge(max_turned, ex.counted(1, 1))
                        if positive(count := ex.counted(H, (1 - RING) * H)):
                            dve.wait_ge(exp_scored, count)
                        dve.tensor_tensor(m.q_shift[:, ex.r], m.q_stack[:, ex.r].bitcast(F32), ps_wide[:], ALU.add).then_inc(shifted, 1)
                    if s == at["split_lo"] and prep.there():
                        dve.wait_ge(hi_ready, prep.counted(2, 2))
                        if positive(count := prep.counted(1, 0)):
                            dve.wait_ge(q_stacked, count)
                        if parts == 1:
                            dve.scalar_tensor_tensor(m.qk_lo[:], m.qk_hi[:].bitcast(F32), m.col[:, 3:4], ps_small[:], ALU.mult, ALU.add).then_inc(lo_ready, 1)
                        else:
                            for which in range(2):
                                ins = dve.scalar_tensor_tensor(m.qk_lo[:, which, :], ps_small[:, which, :], m.col[:, which:which + 1],
                                                               m.qk_hi[:, which, :].bitcast(F32), ALU.add, ALU.subtract)
                            ins.then_inc(lo_ready, 1)
                    if hd == 8 and s == at["copy_v"] and prep.there():
                        dve.wait_ge(v_done, prep.counted(1, 1))
                        if positive(count := prep.counted(NG, (1 - RING) * NG)):
                            dve.wait_ge(weighed, count)
                        src = ps_small[:, 0, 0:NT * HD].rearrange("p (t h d) -> p t h d", t=NT, h=H)
                        bias = m.wide[:, 3:4, :].rearrange("p a (h d) -> p a h d", h=H).to_broadcast([P, NT, H, hd])
                        dve.tensor_tensor(m.v_ones[:, prep.r, :, :, 0:hd], src, bias, ALU.add).then_inc(v_copied, 1)
                    if s == at["divide"] and tail.there():
                        dve.wait_ge(out_turned, tail.counted(1, 1))
                        turned = ps_wide.rearrange("p g s -> p (g s)").rearrange("p (t h c) -> p t h c", t=NT, h=H)
                        if positive(count := tail.counted(1, 0)):
                            dve.wait_ge(divided, count)
                        dve.reciprocal(m.inv_sum[:], turned[:, :, :, hd]).then_inc(inv_done, 1)
                        dve.wait_ge(inv_done, tail.counted(1, 1))
                        if positive(count := tail.counted(1, 0)):
                            dve.wait_ge(norm_turned, count)
                        out = m.out_n[:, :, 0:HD].rearrange("p t (h d) -> p t h d", h=H)
                        dve.tensor_tensor(out, turned[:, :, :, 0:hd], m.inv_sum[:].unsqueeze(3).to_broadcast([P, NT, H, hd]), ALU.mult).then_inc(divided, 1)
                    if s == at["add_out"] and tail.there():
                        dve.wait_ge(projected, tail.counted(1, 1))
                        dve.wait_ge(bias_added, tail.counted(1, 1))
                        if not norm_out and (tail.i is not None or tail.c >= RING):
                            dve.wait_ge(stored[tail.r], tail.back(RING).used(16))
                        if norm_out:
                            if positive(count := tail.counted(NT, 0)):
                                dve.wait_ge(y_done, count)
                        dst = m.y[:] if norm_out else m.y_out[:, tail.r]
                        dve.tensor_tensor(dst, ps_small[:, 0, :].rearrange("p (t d) -> p t d", t=NT), m.x_res[:, tail.r], ALU.add).then_inc(summed, 1)
                        if norm_out:
                            dve.wait_ge(summed, tail.counted(1, 1))
                            norm(tail, m.y, None, m.stats, m.mean_var, m.var_eps, m.rstd,
                                 (stats_done, aggr_done, eps_done, rstd_done, y_done), 0)
                    if s == at["norm_out"] and tail.there() and norm_out:
                        if tail.i is not None or tail.c >= RING:
                            dve.wait_ge(stored[tail.r], tail.back(RING).used(16))
                        norm(tail, m.y, m.y_out[:, tail.r], m.stats, m.mean_var, m.var_eps, m.rstd,
                             (stats_done, aggr_done, eps_done, rstd_done, y_done), 1)

            run_turns(dve, step, first, B, total)


SLOTS_1 = {"split_second": (1, 6, 14, 22), "split": (10, 17, 17, 17), "stats": 0, "norm": 3, "turn_x": 8, "route": 11, "rank": 13, "score": 14, "weigh": 18, "turn_y": 21, "stats_y": 24, "norm_y": 28, "turn_gates": 26}
SLOTS_2 = {"split": (2, 12, 12, 12), "stats": 0, "norm": 0, "turn_x": 0, "route": 1, "score": 2, "turn_y": 4, "stats_y": 5, "rank": 6, "weigh": 11, "turn_gates": 12, "norm_y": 12}


class Links:

    def __init__(self, turn, per):
        self.turn, self.per, self.n = turn, per, 0

    def next(self):
        self.n += 1
        assert self.n <= self.per
        return self.made()

    def made(self):
        return self.turn.counted(self.per, self.n)


BT = 4
TOK = BT * P
NB = B * S // TOK
BRING = 2
LO = 32


def expert_stage(nc, tag, experts, chunks, last_rows, gated, slots, x, x_more, y, w):
    E = experts
    x_v = x.rearrange("b s d -> (b s) d").rearrange("(n t p) d -> n p t d", p=P, t=BT)
    more_v = None if x_more is None else x_more.rearrange("b s d -> (b s) d").rearrange("(n t p) d -> n p t d", p=P, t=BT)
    y_v = y.rearrange("b s d -> (b s) d").rearrange("(n t p) d -> n p t d", p=P, t=BT)
    norm_in = x_more is not None
    NX = 2 if norm_in else 1
    first = 4
    HR = 4
    BEHIND = 2 if gated else 3
    DVE_ROUNDS = 1
    NW = 2 if gated else 1
    gates = chunks - 1 if gated else E
    per_gate = chunks // E if not gated else 1
    CHAIN = 27 if gated else 13
    SCALED = gates if gated else chunks

    def place(c):
        return HR if gated and c == gates else c % HR

    def place_used(c):
        if gated and c == gates:
            return c - chunks
        return c - HR if c >= HR or not gated else c - HR - 1

    def bank(b, c):
        return (b.r * chunks + c) % 2

    with ExitStack() as ctx:
        sem = stage_semaphores(nc, ctx, tag)

        def sb(name, shape, dt=F32):
            return ctx.enter_context(nc.sbuf_tensor(f"{tag}_{name}", shape, dt))

        def psum(name, shape):
            return ctx.enter_context(nc.psum_tensor(f"{tag}_{name}", shape, F32))

        w_raw = sb("w_raw", [P, chunks, NW, P])
        w_hi = sb("w_hi", [P, chunks, NW, P], F32R)
        w_lo = sb("w_lo", [P, chunks, NW, P], F32R)
        if gated:
            w_out = sb("w_out", [P, chunks, D])
            scaled = sb("scaled", [P, 5, TOK])
            mixed = sb("mixed", [P, 4, TOK])
            y_t = sb("y_t", [P, TOK])
        else:
            w_out_hi = sb("w_out_hi", [P, chunks, D], F32R)
            w_out_lo = sb("w_out_lo", [P, chunks, D], F32R)
            hidden_hi = sb("hidden_hi", [P, HR, TOK], F32R)
            hidden_lo = sb("hidden_lo", [P, HR, TOK], F32R)
            gate_wide = sb("gate_wide", [P, 2, TOK])
            y_acc = sb("y_acc", [P, BRING, TOK])
            y_part = sb("y_part", [P, TOK])
        w_gate = sb("w_gate", [P, E])
        b_out = sb("b_out", [P, E])
        b_hidden = sb("b_hidden", [P, chunks])
        wide = sb("wide", [P, 2, D])
        gate_bias = sb("gate_bias", [P, E])
        before = sb("before", [P, E, E])
        ident = sb("ident", [P, P])
        sel = sb("sel", [P, gates, P], F32R)
        neg_half = sb("neg_half", [P, BT])
        x_in = sb("x_in", [P, BRING, BT, D])
        x_res = sb("x_res", [P, 2, BRING, BT, D])
        x_norm = sb("x_norm", [P, BT, D])
        x_t = sb("x_t", [P, TOK])
        x_hi = sb("x_hi", [P, BRING, TOK], F32R)
        x_lo = sb("x_lo", [P, BRING, TOK], F32R)
        gate_t = sb("gate_t", [P, BRING, TOK], F32R)
        gate_rows = sb("gate_rows", [P, BT, P])
        hidden = sb("hidden", [P, HR + 1 if gated else HR, TOK])
        y_sum = sb("y_sum", [P, BT, D])
        y_out = sb("y_out", [P, BRING, BT, D])
        stats = sb("stats", [P, 2, BT, 6])
        mean_var = sb("mean_var", [P, 2, BT + 1, 2])
        var_eps = sb("var_eps", [P, 2, BT])
        rstd = sb("rstd", [P, 2, BT])
        logits = sb("logits", [P, BT, E])
        greater = sb("greater", [P, BT, E, E])
        equal = sb("equal", [P, BT, E, E])
        rank = sb("rank", [P, BT, E])
        chosen = sb("chosen", [P, BT, E])
        shifted = sb("shifted", [P, BT, E])
        weight = sb("weight", [P, BT, E])
        top = sb("top", [P, BT])
        base = sb("base", [P, BT, E])
        total_w = sb("total_w", [P, BT])
        if gated:
            small = sb("small", [P, 8, BT, 4, 2])
            group_sums = sb("group_sums", [P, BT * 4])
            group_ranks = sb("group_ranks", [P, BT * 4])

        ps_h = psum("ps_h", [P, 2 * NW, TOK])
        ps_gate = psum("ps_gate", [P, 1 if gated else 2, TOK])
        ps_y = psum("ps_y", [P, 1 if gated else 2, TOK])
        ps_turn = psum("ps_turn", [P, TOK])
        ps_logits = psum("ps_logits", [P, BT, E])
        GR = 1 if gated else 2

        sel_loaded, loaded_first, loaded, cleared = sem("sel_loaded"), sem("loaded_first"), sem("loaded"), sem("cleared")
        raw_loaded = [sem(f"raw_loaded{n}") for n in range(4)]
        raw_hi, raw_split, second_loaded = sem("raw_hi"), sem("raw_split"), sem("second_loaded")
        x_loaded = [sem(f"x_loaded{r}") for r in range(BRING)]
        res_loaded = [sem(f"res_loaded{r}") for r in range(BRING)]
        stored = [sem(f"stored{r}") for r in range(BRING)]
        xt_done, routed, gates_turned = sem("xt_done"), sem("routed"), sem("gates_turned")
        first_done, spread, second_done = sem("first_done"), sem("spread"), sem("second_done")
        y_turned = sem("y_turned")
        xt_copied, hi_ready, score_done, gates_copied = sem("xt_copied"), sem("hi_ready"), sem("score_done"), sem("gates_copied")
        activated, y_copied = sem("activated"), sem("y_copied")
        lo_ready, to_score, rows_ready = sem("lo_ready"), sem("to_score"), sem("rows_ready")
        mixed_done, scaled_done, chained = sem("mixed_done"), sem("scaled_done"), sem("chained")
        in_stats, in_aggr, in_eps, in_normed = sem("in_stats"), sem("in_aggr"), sem("in_eps"), sem("in_normed")
        summed, out_stats, out_aggr, out_eps, y_done = sem("summed"), sem("out_stats"), sem("out_aggr"), sem("out_eps"), sem("y_done")
        in_rstd, in_scaled, in_ready = sem("in_rstd"), sem("in_scaled"), sem("in_ready")
        raw2_loaded = [sem(f"raw2_loaded{n}") for n in range(4)]
        raw2_hi, raw2_split = sem("raw2_hi"), sem("raw2_split")
        rounded, dve_rounded, gate_ready, rest_done, weighed, y_added = sem("rounded"), sem("dve_rounded"), sem("gate_ready"), sem("rest_done"), sem("weighed"), sem("y_added")
        res_ready, out_rstd = sem("res_ready"), sem("out_rstd")

        block = ctx.enter_context(nc.Block())

        PIECE = -(-chunks // 4)
        pieces = [range(c, min(c + PIECE, chunks)) for c in range(0, chunks, PIECE)]

        def piece_of(weights, n):
            piece = weights[:, pieces[n].start:pieces[n].stop]
            return piece.rearrange("p c w f -> p (c w) f") if len(piece.shape) == 4 else piece

        later = [(w_gate[:], w["gate"]), (before[:], w["before"]), (gate_bias[:], w["gate_bias"]), (b_hidden[:], w["b_hidden"]),
                 (b_out[:], w["b_out"])]
        LOADED = 16 * len(later)

        @block.sync
        def _(sp):
            for dst, src in ((ident[:], w["ident"]), (wide[:], w["wide"])):
                sp.dma_start(dst, src).then_inc(loaded_first, 16)

            def io_step(t):
                if t.there():
                    if norm_in:
                        if positive(count := t.counted(BT, (1 - BRING) * BT)):
                            sp.wait_ge(in_normed, count)
                    else:
                        if positive(count := t.counted(1, 1 - BRING)):
                            sp.wait_ge(xt_done, count)
                    sp.dma_start(x_in[:, t.r], t.of(x_v)).then_inc(x_loaded[t.r], 16)
                if not gated and t.i is None and t.c == 1:
                    for n in range(len(pieces)):
                        sp.wait_ge(raw_split, n + 1)
                        sp.dma_start(piece_of(w_raw, n), piece_of(w["second"], n)).then_inc(raw2_loaded[n], 16)
                b = t.back(2)
                if b.there():
                    if positive(count := b.counted(1, 1 - BRING)):
                        sp.wait_ge(summed, count)
                    sp.dma_start(x_res[:, 0, b.r], b.of(x_v)).then_inc(res_loaded[b.r], 16)
                    if norm_in:
                        sp.dma_start(x_res[:, 1, b.r], b.of(more_v)).then_inc(res_loaded[b.r], 16)
                b = t.back(3)
                if b.there():
                    sp.wait_ge(y_done, b.counted(BT, BT))
                    sp.dma_start(b.of(y_v), y_out[:, b.r]).then_inc(stored[b.r], 16)

            run_turns(sp, io_step, first, NB, NB + 3, BRING)
            for r in range(BRING):
                sp.wait_ge(stored[r], 16 * len(range(r, NB, BRING)))

        @block.gpsimd
        def _(pool):
            pool.dma_start(sel[:], w["sel"].bitcast(F32R)).then_inc(sel_loaded, 16)
            pool.memset(neg_half[:], -0.5).then_inc(cleared, 1)
            pool.memset(gate_rows[:], 0.0).then_inc(cleared, 1)
            pool.memset(base[:], float(np.e)).then_inc(cleared, 1)
            pool.wait_ge(cleared, 3)
            pool.wait_ge(loaded_first, 16 * 2)

            def step(t):
                if norm_in and t.there():
                    pool.wait_ge(in_eps, t.counted(1, 1))
                    pool.tensor_tensor(rstd[:, 0], var_eps[:, 0], neg_half[:], ALU.pow).then_inc(in_rstd, 1)
                    pool.wait_ge(in_normed, t.counted(BT, BT))
                    pool.tensor_tensor(x_norm[:], x_norm[:], wide[:, 0:1, :].to_broadcast([P, BT, D]), ALU.mult).then_inc(in_scaled, 1)
                    pool.wait_ge(in_scaled, t.counted(1, 1))
                    pool.tensor_tensor(x_norm[:], x_norm[:], wide[:, 1:2, :].to_broadcast([P, BT, D]), ALU.add).then_inc(in_ready, 1)
                if not gated and t.there():
                    pool.wait_ge(to_score, t.counted(1, 1))
                    pool.tensor_tensor(weight[:], base[:], shifted[:], ALU.pow).then_inc(score_done, 1)
                b = t.back(2)
                if b.there():
                    if norm_in:
                        pool.wait_ge(res_loaded[b.r], b.used(16 * NX))
                        pool.tensor_tensor(x_res[:, 0, b.r], x_res[:, 0, b.r], x_res[:, 1, b.r], ALU.add).then_inc(res_ready, 1)
                    pool.wait_ge(out_eps, b.counted(1, 1))
                    pool.tensor_tensor(rstd[:, 1], var_eps[:, 1], neg_half[:], ALU.pow).then_inc(out_rstd, 1)

            run_turns(pool, step, first, NB, NB + 2, BRING)

        @block.tensor
        def _(pe):
            def first_products(b, c):
                if c == 0:
                    pe.wait_ge(lo_ready, b.counted(1, 1))
                if gated:
                    if positive(count := b.counted(chunks, c - 1)):
                        pe.wait_ge(mixed_done, count)
                else:
                    if positive(count := b.counted(chunks, c - 1)):
                        pe.wait_ge(activated, count)
                if b.i is None and b.c == 0 and c % PIECE == 0:
                    pe.wait_ge(raw_split, c // PIECE + 1)
                rows = P if c < chunks - 1 else last_rows
                for k in range(NW):
                    out = ps_h[0:rows, NW * bank(b, c) + k, :]
                    pe.matmul(out, w_hi[:, c, k, 0:rows], x_hi[:, b.r], start=True, stop=False)
                    pe.matmul(out, w_hi[:, c, k, 0:rows], x_lo[:, b.r], start=False, stop=False)
                    ins = pe.matmul(out, w_lo[:, c, k, 0:rows], x_hi[:, b.r], start=False, stop=True)
                ins.then_inc(first_done, 1)

            def spread_gate(b, g):
                if g == 0:
                    pe.wait_ge(gates_copied, b.counted(1, 1))
                if gated:
                    if positive(count := b.counted(SCALED, g)):
                        pe.wait_ge(scaled_done, count)
                else:
                    if positive(count := b.counted(E, g - 1)):
                        pe.wait_ge(gate_ready, count)
                pe.matmul(ps_gate[:, g % GR, :], sel[:, g, :], gate_t[:, b.r], start=True, stop=True).then_inc(spread, 1)

            def second_product(b, c):
                if gated:
                    if c == 0:
                        if positive(count := b.counted(1, 0)):
                            pe.wait_ge(y_copied, count)
                        if b.i is None and b.c == 0:
                            pe.wait_ge(second_loaded, 16)
                    if c == gates:
                        pe.wait_ge(mixed_done, b.counted(chunks, c + 1))
                    else:
                        pe.wait_ge(scaled_done, b.counted(SCALED, c + 1))
                    rows = P if c < chunks - 1 else last_rows
                    pe.matmul(ps_y[:, 0, :], w_out[0:rows, c, :], scaled[0:rows, place(c), :], start=(c == 0), stop=(c == chunks - 1)).then_inc(second_done, 1)
                else:
                    g, first_of, last_of = c // per_gate, c % per_gate == 0, c % per_gate == per_gate - 1
                    if first_of:
                        if positive(count := b.counted(E, g - 1)):
                            pe.wait_ge(weighed, count)
                    if b.i is None and b.c == 0 and c % PIECE == 0:
                        pe.wait_ge(raw2_split, c // PIECE + 1)
                    pe.wait_ge(rest_done, b.counted(chunks, c + 1))
                    out = ps_y[:, g % 2, :]
                    pe.matmul(out, w_out_hi[:, c, :], hidden_hi[:, c % HR, :], start=first_of, stop=False)
                    pe.matmul(out, w_out_lo[:, c, :], hidden_hi[:, c % HR, :], start=False, stop=False)
                    pe.matmul(out, w_out_hi[:, c, :], hidden_lo[:, c % HR, :], start=False, stop=last_of).then_inc(second_done, 1)

            def step(t):
                new, cur, old = t, t.back(1), t.back(2)
                for s in range(chunks):
                    if cur.there():
                        if gated:
                            if s > 0:
                                spread_gate(cur, s - 1)
                            first_products(cur, s)
                        else:
                            if s % per_gate == 0:
                                spread_gate(cur, s // per_gate)
                            first_products(cur, s)
                    if s < BEHIND and old.there():
                        second_product(old, chunks - BEHIND + s)
                    if s >= BEHIND and cur.there():
                        second_product(cur, s - BEHIND)
                    if s == slots["turn_y"] and old.there():
                        if gated:
                            pe.wait_ge(y_copied, old.counted(1, 1))
                        else:
                            pe.wait_ge(y_added, old.counted(E - 1, E - 1))
                        pe.wait_ge(gates_copied, old.counted(1, 2))
                        pe.wait_ge(lo_ready, old.counted(1, 3))
                        for i in range(BT):
                            src = y_t[:, i * P:i * P + P] if gated else y_acc[:, old.r, i * P:i * P + P]
                            ins = pe.transpose(ps_turn[:, i * P:i * P + P], src, ident[:])
                        ins.then_inc(y_turned, 1)
                    if s == slots["turn_x"] and new.there():
                        if norm_in:
                            pe.wait_ge(in_ready, new.counted(1, 1))
                        else:
                            pe.wait_ge(x_loaded[new.r], new.used(16))
                        if positive(count := new.counted(1, 0)):
                            pe.wait_ge(gates_copied, count)
                        for i in range(BT):
                            src = x_norm[:, i, :] if norm_in else x_in[:, new.r, i, :]
                            ins = pe.transpose(ps_turn[:, i * P:i * P + P], src, ident[:])
                        ins.then_inc(xt_done, 1)
                    if s == slots["route"] and new.there():
                        if new.i is None and new.c == 0:
                            pe.wait_ge(loaded, LOADED)
                            pe.wait_ge(sel_loaded, 16)
                        pe.wait_ge(xt_copied, new.counted(1, 1))
                        for i in range(BT):
                            ins = pe.matmul(ps_logits[:, i, :], x_t[:, i * P:i * P + P], w_gate[:], start=True, stop=True)
                        ins.then_inc(routed, 1)
                    if s == slots["turn_gates"] and new.there():
                        pe.wait_ge(rows_ready, new.counted(1, 1))
                        pe.wait_ge(lo_ready, new.counted(1, 1))
                        if positive(count := new.counted(1, -1)):
                            pe.wait_ge(summed, count)
                        for i in range(BT):
                            ins = pe.transpose(ps_turn[:, i * P:i * P + P], gate_rows[:, i, :], ident[:])
                        ins.then_inc(gates_turned, 1)

            pe.wait_ge(loaded_first, 16 * 2)
            run_turns(pe, step, first, NB, NB + 2, BRING)

        @block.scalar
        def _(act):
            def activate(b, c):
                act.wait_ge(first_done, b.counted(chunks, c + 1))
                rows = P if c < chunks - 1 else last_rows
                if positive(count := b.counted(chunks, place_used(c) + 1)):
                    act.wait_ge(mixed_done if gated else rest_done, count)
                if gated:
                    act.activation(hidden[0:rows, place(c), :], ps_h[0:rows, NW * bank(b, c), :], ACT.Silu).then_inc(activated, 1)
                else:
                    act.activation(hidden[:, place(c), :], ps_h[:, bank(b, c), :], ACT.Gelu, bias=b_hidden[:, c:c + 1]).then_inc(activated, 1)
                    if c % 4 != DVE_ROUNDS:
                        act.wait_ge(activated, b.counted(chunks, c + 1))
                        if positive(count := b.counted(chunks, c + 1 - HR)):
                            act.wait_ge(second_done, count)
                        act.activation(hidden_hi[:, c % HR, :], hidden[:, c % HR, :], ACT.Copy).then_inc(rounded, 1)

            def copy_gate(b, g):
                act.wait_ge(spread, b.counted(gates, g + 1))
                if positive(count := b.counted(E, g - 1)):
                    act.wait_ge(weighed, count)
                act.activation(gate_wide[:, g % 2, :], ps_gate[:, g % 2, :], ACT.Copy).then_inc(gate_ready, 1)

            def step(t):
                new, cur, old = t, t.back(1), t.back(2)
                for s in range(chunks):
                    if cur.there():
                        activate(cur, s)
                        if not gated and s % per_gate == 1:
                            copy_gate(cur, s // per_gate)
                    if gated and s == BEHIND and old.there():
                        act.wait_ge(second_done, old.counted(chunks, chunks))
                        if positive(count := old.counted(1, 0)):
                            act.wait_ge(y_turned, count)
                        act.activation(y_t[:], ps_y[:, 0, :], ACT.Copy).then_inc(y_copied, 1)
                    if s == slots["turn_x"] + 1 and new.there():
                        act.wait_ge(xt_done, new.counted(1, 1))
                        if positive(count := new.counted(1, 0)):
                            act.wait_ge(routed, count)
                        act.activation(x_t[:], ps_turn[:], ACT.Copy).then_inc(xt_copied, 1)
                        if positive(count := new.counted(chunks, (1 - BRING) * chunks)):
                            act.wait_ge(first_done, count)
                        act.activation(x_hi[:, new.r], ps_turn[:], ACT.Copy).then_inc(hi_ready, 1)
                    if s == slots["score"] and new.there() and new.i is None and new.c == 0:
                        act.wait_ge(loaded, LOADED)
                    if gated and s == slots["score"] and new.there():
                        act.wait_ge(to_score, new.counted(1, 1))
                        act.activation(shifted[:], logits[:], ACT.Sigmoid).then_inc(score_done, 1)
                    if s == min(slots["turn_gates"] + 1, chunks - 1) and new.there():
                        act.wait_ge(gates_turned, new.counted(1, 1))
                        if positive(count := new.counted(gates, (1 - BRING) * gates)):
                            act.wait_ge(spread, count)
                        act.activation(gate_t[:, new.r], ps_turn[:], ACT.Copy).then_inc(gates_copied, 1)
                    for n in range(len(pieces)):
                        if s == slots["split"][n] and new.i is None and new.c == 0:
                            act.wait_ge(raw_loaded[n], 16)
                            act.activation(piece_of(w_hi, n), piece_of(w_raw, n), ACT.Copy).then_inc(raw_hi, 1)
                        if not gated and s == slots["split_second"][n] and cur.i is None and cur.c == 0:
                            act.wait_ge(raw2_loaded[n], 16)
                            act.activation(piece_of(w_out_hi, n), piece_of(w_raw, n), ACT.Copy).then_inc(raw2_hi, 1)

            for dst, src in later:
                act.dma_start(dst, src).then_inc(loaded, 16)
            for n in range(len(pieces)):
                act.dma_start(piece_of(w_raw, n), piece_of(w["first"], n)).then_inc(raw_loaded[n], 16)
            if gated:
                act.dma_start(w_out[:], w["second"]).then_inc(second_loaded, 16)
            run_turns(act, step, first, NB, NB + 2, BRING)

        @block.vector
        def _(dve):
            dve.wait_ge(cleared, 3)

            def norm_stats(b, src, k, s_stats, s_aggr, s_eps, s_done):
                if positive(count := b.counted(BT, 0)):
                    dve.wait_ge(s_done, count)
                for i in range(BT):
                    dve.bn_stats(stats[:, k, i, :], src[:, i, :]).then_inc(s_stats, 1)
                dve.wait_ge(s_stats, b.counted(BT, BT))
                dve.tensor_copy(mean_var[:, k, BT, 0:1], stats[:, k, 0, 1:2]).then_inc(s_aggr, 1)
                for i in range(BT):
                    dve.bn_aggr(mean_var[:, k, i, :], stats[:, k, i, :]).then_inc(s_aggr, 1)
                dve.wait_ge(s_aggr, b.counted(BT + 1, BT + 1))
                dve.tensor_scalar(var_eps[:, k], mean_var[:, k, 0:BT, 1], EPS, None, ALU.add).then_inc(s_eps, 1)

            def norm_apply(b, src, dst, k, s_rstd, s_done):
                dve.wait_ge(s_rstd, b.counted(1, 1))
                for i in range(BT):
                    dve.tensor_scalar(dst[:, i, :], src[:, i, :], mean_var[:, k, i, 0:1], rstd[:, k, i:i + 1],
                                      ALU.subtract, ALU.mult).then_inc(s_done, 1)

            def rank_of(values, n, outer, out, links, parts=range(5)):
                shape = [P, outer, n, n]
                gt = greater.rearrange("p t e f -> p (t e f)")[:, 0:outer * n * n].rearrange("p (t e f) -> p t e f", t=outer, e=n)
                eq = equal.rearrange("p t e f -> p (t e f)")[:, 0:outer * n * n].rearrange("p (t e f) -> p t e f", t=outer, e=n)
                others, own = values.unsqueeze(2).to_broadcast(shape), values.unsqueeze(3).to_broadcast(shape)
                if 0 in parts:
                    dve.wait_ge(chained, links.made())
                    dve.tensor_tensor(gt, others, own, ALU.is_gt).then_inc(chained, 1)
                    links.next()
                if 1 in parts:
                    dve.tensor_tensor(eq, others, own, ALU.is_equal).then_inc(chained, 1)
                    links.next()
                if 2 in parts:
                    dve.wait_ge(chained, links.made())
                    dve.tensor_tensor(eq, eq, before[:, 0:n, 0:n].unsqueeze(1).to_broadcast(shape), ALU.mult).then_inc(chained, 1)
                    links.next()
                if 3 in parts:
                    dve.wait_ge(chained, links.made())
                    dve.tensor_tensor(gt, gt, eq, ALU.add).then_inc(chained, 1)
                    links.next()
                if 4 in parts:
                    dve.wait_ge(chained, links.made())
                    dve.tensor_reduce(out, gt, AX.X, ALU.add).then_inc(chained, 1)
                    links.next()

            def bc(a):
                return a.unsqueeze(2).to_broadcast([P, BT, E])

            def route_first(b, links):
                if b.i is None and b.c == 0:
                    dve.wait_ge(loaded, LOADED)
                dve.wait_ge(routed, b.counted(1, 1))
                if gated:
                    dve.tensor_copy(logits[:], ps_logits[:]).then_inc(to_score, 1)
                else:
                    dve.tensor_copy(logits[:], ps_logits[:]).then_inc(chained, 1)
                    dve.wait_ge(chained, links.next())
                    dve.tensor_reduce(top[:], logits[:], AX.X, ALU.max).then_inc(chained, 1)
                    dve.wait_ge(chained, links.next())
                    dve.tensor_tensor(shifted[:], logits[:], bc(top[:]), ALU.subtract).then_inc(to_score, 1)

            def col(k):
                return small[:, k].rearrange("p t g a -> p (t g) a")[:, :, 0]

            def route_groups(b, links):
                dve.wait_ge(score_done, b.counted(1, 1))
                dve.tensor_tensor(logits[:], shifted[:], gate_bias[:].unsqueeze(1).to_broadcast([P, BT, E]), ALU.add).then_inc(chained, 1)
                dve.wait_ge(chained, links.next())
                pairs = logits.rearrange("p t (g a c) -> p (t g) a c", g=4, a=2)
                hi, lo = small[:, 0].rearrange("p t g a -> p (t g) a"), small[:, 1].rearrange("p t g a -> p (t g) a")

                dve.tensor_tensor(hi, pairs[:, :, :, 0], pairs[:, :, :, 1], ALU.max)
                dve.tensor_tensor(lo, pairs[:, :, :, 0], pairs[:, :, :, 1], ALU.min).then_inc(chained, 1)
                dve.wait_ge(chained, links.next())
                dve.tensor_tensor(col(2), hi[:, :, 0], hi[:, :, 1], ALU.max)
                dve.tensor_tensor(col(3), hi[:, :, 0], hi[:, :, 1], ALU.min)
                dve.tensor_tensor(col(4), lo[:, :, 0], lo[:, :, 1], ALU.max).then_inc(chained, 1)
                dve.wait_ge(chained, links.next())
                dve.tensor_tensor(col(5), col(3), col(4), ALU.max).then_inc(chained, 1)
                dve.wait_ge(chained, links.next())
                dve.tensor_tensor(group_sums[:], col(2), col(5), ALU.add).then_inc(chained, 1)
                dve.wait_ge(chained, links.next())

            def route_mask(links):
                rank_of(group_sums.rearrange("p (t g) -> p t g", g=4), 4, BT, group_ranks.rearrange("p (t g) -> p t g", g=4), links)
                dve.wait_ge(chained, links.made())
                dve.tensor_scalar(col(6), group_ranks[:], 2.0, None, ALU.is_lt).then_inc(chained, 1)
                dve.wait_ge(chained, links.next())
                dve.tensor_scalar(col(7), col(6), 1.0, -MASKED, ALU.subtract, ALU.mult).then_inc(chained, 1)
                dve.wait_ge(chained, links.next())
                by_group = logits.rearrange("p t (g c) -> p (t g) c", g=4)
                dve.tensor_tensor(by_group, by_group, col(6).unsqueeze(2).to_broadcast([P, BT * 4, 4]), ALU.mult).then_inc(chained, 1)
                dve.wait_ge(chained, links.next())
                dve.tensor_tensor(by_group, by_group, col(7).unsqueeze(2).to_broadcast([P, BT * 4, 4]), ALU.add).then_inc(chained, 1)
                dve.wait_ge(chained, links.next())

            def route_weights(b, links):
                if gated:
                    dve.wait_ge(chained, links.made())
                    dve.tensor_scalar(chosen[:], rank[:], 4.0, None, ALU.is_lt).then_inc(chained, 1)
                    dve.wait_ge(chained, links.next())
                    dve.tensor_tensor(weight[:], shifted[:], chosen[:], ALU.mult).then_inc(chained, 1)
                    dve.wait_ge(chained, links.next())
                    dve.tensor_reduce(total_w[:], weight[:], AX.X, ALU.add).then_inc(chained, 1)
                    dve.wait_ge(chained, links.next())
                    dve.tensor_scalar(total_w[:], total_w[:], 1e-20, None, ALU.add).then_inc(chained, 1)
                    dve.wait_ge(chained, links.next())
                    dve.reciprocal(total_w[:], total_w[:]).then_inc(chained, 1)
                    dve.wait_ge(chained, links.next())
                    dve.tensor_tensor(weight[:], weight[:], bc(total_w[:]), ALU.mult).then_inc(chained, 1)
                    dve.wait_ge(chained, links.next())
                    dve.tensor_scalar(weight[:], weight[:], 2.5, None, ALU.mult).then_inc(chained, 1)
                    dve.wait_ge(chained, links.next())
                else:
                    dve.wait_ge(chained, links.made())
                    dve.tensor_scalar(chosen[:], rank[:], 2.0, None, ALU.is_lt).then_inc(chained, 1)
                    dve.wait_ge(chained, links.next())
                    dve.wait_ge(score_done, b.counted(1, 1))
                    dve.tensor_tensor(weight[:], weight[:], chosen[:], ALU.mult).then_inc(chained, 1)
                    dve.wait_ge(chained, links.next())
                    dve.tensor_reduce(total_w[:], weight[:], AX.X, ALU.add).then_inc(chained, 1)
                    dve.wait_ge(chained, links.next())
                    dve.reciprocal(total_w[:], total_w[:]).then_inc(chained, 1)
                    dve.wait_ge(chained, links.next())
                    dve.tensor_tensor(weight[:], weight[:], bc(total_w[:]), ALU.mult).then_inc(chained, 1)
                    dve.wait_ge(chained, links.next())
                if positive(count := b.counted(1, 0)):
                    dve.wait_ge(gates_turned, count)
                dve.tensor_copy(gate_rows[:, :, 0:E].bitcast(F32R), weight[:]).then_inc(chained, 1)
                dve.wait_ge(chained, links.next())
                dve.tensor_tensor(gate_rows[:, :, LO:LO + E].bitcast(F32R), weight[:], gate_rows[:, :, 0:E], ALU.subtract).then_inc(rows_ready, 1)
                assert links.n == CHAIN, links.n

            def mix(b, c):
                dve.wait_ge(activated, b.counted(chunks, c + 1))
                rows = P if c < chunks - 1 else last_rows
                if positive(count := b.counted(chunks, place_used(c) + 1)):
                    dve.wait_ge(second_done, count)
                dst = mixed[:, place(c), :] if c < gates else scaled[0:rows, place(c), :]
                dve.tensor_tensor(dst, ps_h[0:rows, NW * bank(b, c) + 1, :], hidden[0:rows, place(c), :], ALU.mult).then_inc(mixed_done, 1)

            def scale(b, c):
                dve.wait_ge(mixed_done, b.counted(chunks, c + 1))
                dve.wait_ge(spread, b.counted(gates, c + 1))
                dve.tensor_tensor(scaled[:, place(c), :], mixed[:, place(c), :], ps_gate[:, 0, :], ALU.mult).then_inc(scaled_done, 1)

            def rest(b, c):
                if positive(count := b.counted(chunks, c + 1 - HR)):
                    dve.wait_ge(second_done, count)
                if c % 4 == DVE_ROUNDS:
                    dve.wait_ge(activated, b.counted(chunks, c + 1))
                    dve.tensor_copy(hidden_hi[:, c % HR, :], hidden[:, c % HR, :]).then_inc(dve_rounded, 1)
                    dve.wait_ge(dve_rounded, b.counted(chunks // 4, c // 4 + 1))
                else:
                    dve.wait_ge(rounded, b.counted(chunks - chunks // 4, c + 1 - (c + 3 - DVE_ROUNDS + 1) // 4))
                dve.tensor_tensor(hidden_lo[:, c % HR, :], hidden[:, c % HR, :], hidden_hi[:, c % HR, :].bitcast(F32), ALU.subtract).then_inc(rest_done, 1)

            def weigh(b, g):
                dve.wait_ge(second_done, b.counted(chunks, (g + 1) * per_gate))
                dve.wait_ge(gate_ready, b.counted(E, g + 1))
                if g == 0:
                    if positive(count := b.counted(1, 1 - BRING)):
                        dve.wait_ge(y_turned, count)
                else:
                    if positive(count := b.counted(E - 1, g - 1)):
                        dve.wait_ge(y_added, count)
                dst = y_acc[:, b.r, :] if g == 0 else y_part[:]
                dve.scalar_tensor_tensor(dst, ps_y[:, g % 2, :], b_out[:, g:g + 1], gate_wide[:, g % 2, :], ALU.add, ALU.mult).then_inc(weighed, 1)
                if g > 0:
                    dve.wait_ge(weighed, b.counted(E, g + 1))
                    dve.tensor_tensor(y_acc[:, b.r, :], y_acc[:, b.r, :], y_part[:], ALU.add).then_inc(y_added, 1)

            def step(t):
                new, cur, old = t, t.back(1), t.back(2)
                links = Links(new, CHAIN)
                for s in range(chunks):
                    if gated and cur.there():
                        if s > 0:
                            scale(cur, s - 1)
                        mix(cur, s)
                    if not gated and cur.there():
                        rest(cur, s)
                        behind = s - per_gate - BEHIND
                        if behind >= 0 and behind % per_gate == 0:
                            weigh(cur, behind // per_gate)
                    if not gated and s == BEHIND and old.there():
                        weigh(old, E - 1)
                    if norm_in and s == slots["stats"] and new.there():
                        dve.wait_ge(x_loaded[new.r], new.used(16))
                        norm_stats(new, x_in[:, new.r], 0, in_stats, in_aggr, in_eps, in_normed)
                    if norm_in and s == slots["norm"] and new.there():
                        if positive(count := new.counted(1, 0)):
                            dve.wait_ge(xt_done, count)
                        norm_apply(new, x_in[:, new.r], x_norm, 0, in_rstd, in_normed)
                    if s == slots["turn_x"] + 1 and new.there():
                        dve.wait_ge(hi_ready, new.counted(1, 1))
                        if positive(count := new.counted(chunks, (1 - BRING) * chunks)):
                            dve.wait_ge(first_done, count)
                        dve.tensor_tensor(x_lo[:, new.r], ps_turn[:], x_hi[:, new.r].bitcast(F32), ALU.subtract).then_inc(lo_ready, 1)
                    if s == slots["route"] + 1 and new.there():
                        route_first(new, links)
                    if gated and s == slots["score"] + 1 and new.there():
                        route_groups(new, links)
                    if gated and s == slots["score"] + 2 and new.there():
                        route_mask(links)
                    if slots["rank"] <= s < slots["rank"] + 5 and new.there():
                        rank_of(logits[:], E, BT, rank[:], links, [s - slots["rank"]])
                    if s == slots["weigh"] and new.there():
                        route_weights(new, links)
                    for n in range(len(pieces)):
                        if s == slots["split"][n] and new.i is None and new.c == 0:
                            dve.wait_ge(raw_hi, n + 1)
                            dve.tensor_tensor(piece_of(w_lo, n), piece_of(w_raw, n), piece_of(w_hi, n).bitcast(F32), ALU.subtract).then_inc(raw_split, 1)
                        if not gated and s == slots["split_second"][n] and cur.i is None and cur.c == 0:
                            dve.wait_ge(raw2_hi, n + 1)
                            dve.tensor_tensor(piece_of(w_out_lo, n), piece_of(w_raw, n), piece_of(w_out_hi, n).bitcast(F32), ALU.subtract).then_inc(raw2_split, 1)
                    if s == slots["turn_y"] + 1 and old.there():
                        dve.wait_ge(y_turned, old.counted(1, 1))
                        if norm_in:
                            dve.wait_ge(res_ready, old.counted(1, 1))
                        else:
                            dve.wait_ge(res_loaded[old.r], old.used(16))
                        if positive(count := old.counted(BT, 0)):
                            dve.wait_ge(y_done, count)
                        dve.tensor_tensor(y_sum[:], ps_turn.rearrange("p (t d) -> p t d", t=BT), x_res[:, 0, old.r], ALU.add).then_inc(summed, 1)
                    if s == slots["stats_y"] and old.there():
                        dve.wait_ge(summed, old.counted(1, 1))
                        norm_stats(old, y_sum, 1, out_stats, out_aggr, out_eps, y_done)
                    if s == slots["norm_y"] and old.there():
                        if old.i is not None or old.c >= BRING:
                            dve.wait_ge(stored[old.r], old.back(BRING).used(16))
                        norm_apply(old, y_sum, y_out[:, old.r], 1, out_rstd, y_done)

            run_turns(dve, step, first, NB, NB + 2, BRING)


def stack_selection(hd):
    parts = 1 if hd == 4 else 2
    sel = np.zeros((P, 2, parts, NG, P), np.float32)
    for which, slots in enumerate(((0, 0, 1), (0, 1, 0))):
        for h in range(H):
            g = h % GH
            for slot, part in enumerate(slots):
                for d in range(hd):
                    src = h * hd + d + (part * H * hd if parts == 1 else 0)
                    sel[src, which, part if parts == 2 else 0, h // GH, ROWS * g + slot * hd + d] = 1
    return sel.reshape(P, -1)


def columns(hd, bias_q=None, bias_k=None):
    col = np.zeros((P, 8), np.float32)
    if bias_q is not None:
        col[:, 0], col[:, 1] = bias_q, bias_k
    for g in range(GH):
        col[ROWS * g + 3 * hd:ROWS * g + 3 * hd + 2, 2] = 1
    col[P // 2:, 3] = -1
    return col


def attention_layout(hd, q_t, k_t, v_t, o_t, bias_q=None, bias_k=None, bias_v=None, bias_o=None, norm_w=None, norm_b=None):
    HD = H * hd
    qk = np.zeros((P, 2, P), np.float32)
    for which, wt in enumerate((q_t, k_t)):
        for copy in range(P // HD):
            qk[0:wt.shape[0], which, copy * HD:(copy + 1) * HD] = wt
    v = np.zeros((P, HD), np.float32)
    v[0:v_t.shape[0]] = v_t
    wide = np.zeros((P, 4, D), np.float32)
    for n, row in enumerate((bias_o, norm_w, norm_b, bias_v)):
        if row is not None:
            wide[:, n, :] = row[None, :]
    mask = np.zeros((P, P), np.float32)
    mask[np.triu_indices(P, 1)] = MASKED
    return {"qk": qk, "v": v, "o": np.ascontiguousarray(o_t), "sel": stack_selection(hd), "col": columns(hd, bias_q, bias_k),
            "wide": wide, "ident": np.eye(P, dtype=np.float32), "mask": mask}


def expert_layout(first_t, second_t, gate_t, gate_bias=None, b_hidden=None, b_out=None, norm_w=None, norm_b=None):
    E = gate_t.shape[1]
    units = first_t[0].shape[1]
    chunks = -(-units // P)
    gated = len(first_t) == 2
    first = np.zeros((P, chunks, len(first_t), P), np.float32)
    for k, wt in enumerate(first_t):
        for c in range(chunks):
            n = min(P, units - c * P)
            first[:, c, k, 0:n] = wt[:, c * P:c * P + n]
    second = np.zeros((P, chunks, D), np.float32)
    for c in range(chunks):
        n = min(P, units - c * P)
        second[0:n, c, :] = second_t[c * P:c * P + n]
    gates = chunks - 1 if gated else E
    sel = np.zeros((P, gates, P), np.float32)
    for g in range(gates):
        for j in range(P):
            e = (g * P + j) * E // (gates * P) if gated else g
            sel[e, g, j] = sel[LO + e, g, j] = 1
    wide = np.zeros((P, 2, D), np.float32)
    for n, row in enumerate((norm_w, norm_b)):
        if row is not None:
            wide[:, n, :] = row[None, :]
    out = {"first": first, "second": second, "gate": np.ascontiguousarray(gate_t), "wide": wide, "sel": sel,
           "ident": np.eye(P, dtype=np.float32), "before": np.broadcast_to(np.tri(E, k=-1, dtype=np.float32), (P, E, E)).copy(),
           "gate_bias": np.zeros((P, E), np.float32), "b_hidden": np.zeros((P, chunks), np.float32), "b_out": np.zeros((P, E), np.float32)}
    if gate_bias is not None:
        out["gate_bias"][:] = gate_bias[None, :]
    if b_hidden is not None:
        out["b_hidden"][:] = b_hidden.reshape(chunks, P).T
    if b_out is not None:
        out["b_out"][:] = b_out.T
    return out


def two_layers(nc, x, y, stage_inputs):
    between = [nc.dram_tensor(f"after_stage_{n}", (B, S, D), F32, kind="Internal").ap() for n in range(4)]
    a, b, e1, c, e2 = stage_inputs
    with nc.sbuf_tensor("k_blocks", [P, RING, NG, GH, S], F32R) as k_blocks:
        attention_stage(nc, "a", k_blocks, hd=4, causal=False, norm_in=False, norm_out=True, clear_blocks=True, x=x, y=between[0], w=a)
        attention_stage(nc, "b", k_blocks, hd=8, causal=True, norm_in=True, norm_out=False, clear_blocks=False, x=between[0], y=between[1], w=b)
        expert_stage(nc, "e1", experts=8, chunks=32, last_rows=P, gated=False, slots=SLOTS_1, x=between[1], x_more=between[0], y=between[2], w=e1)
        attention_stage(nc, "c", k_blocks, hd=8, causal=True, norm_in=False, norm_out=True, clear_blocks=False, x=between[2], y=between[3], w=c)
        expert_stage(nc, "e2", experts=16, chunks=13, last_rows=96, gated=True, slots=SLOTS_2, x=between[3], x_more=None, y=y, w=e2)


def layouts(i):
    qkv_b, bias_b = i["L0_ffn_Wqkv"], i["L0_ffn_bqkv"]
    qkv_c, bias_c = i["L1_attn_W_qkv"].T, i["L1_attn_b_qkv"]
    q, k, v = slice(0, D), slice(D, 2 * D), slice(2 * D, 3 * D)

    def units(w):
        return w.transpose(0, 2, 1).reshape(-1, D)

    a = attention_layout(4, i["L0_attn_Wq"].T, i["L0_attn_Wk"].T, i["L0_attn_Wv"].T, i["L0_attn_Wo"].T, bias_o=i["L0_attn_bo"])
    b = attention_layout(8, qkv_b[:, q], qkv_b[:, k], qkv_b[:, v], i["L0_ffn_Wo"], bias_b[q], bias_b[k], bias_b[v], i["L0_ffn_bo"],
                         i["L0_ffn_ln1_w"], i["L0_ffn_ln1_b"])
    e1 = expert_layout([i["L0_ffn_fc1_w"].reshape(-1, D).T], units(i["L0_ffn_fc2_w"]), i["L0_ffn_gate_W"],
                       b_hidden=i["L0_ffn_fc1_b"].reshape(-1), b_out=i["L0_ffn_fc2_b"], norm_w=i["L0_ffn_ln2_w"], norm_b=i["L0_ffn_ln2_b"])
    c = attention_layout(8, qkv_c[:, q], qkv_c[:, k], qkv_c[:, v], i["L1_attn_W_o"].T, bias_c[q], bias_c[k], bias_c[v], i["L1_attn_b_o"])
    gate = np.concatenate([i["L1_ffn_w1"].reshape(-1, D), i["L1_ffn_ws1"]]).T
    up = np.concatenate([i["L1_ffn_w3"].reshape(-1, D), i["L1_ffn_ws3"]]).T
    down = np.concatenate([units(i["L1_ffn_w2"]), i["L1_ffn_ws2"].T])
    e2 = expert_layout([gate, up], down, i["L1_ffn_gate_w"].T, gate_bias=i["L1_ffn_gate_bias"])
    return {"a": a, "b": b, "e1": e1, "c": c, "e2": e2}


def kernel(**inputs):
    import concourse.bacc as bacc
    from concourse.bass_utils import run_bass_kernel_spmd

    nc = bacc.Bacc("TRN2", target_bir_lowering=False, num_devices=1)
    arrays = {name: np.asarray(value) for name, value in inputs.items()}
    fed = {"x": np.ascontiguousarray(arrays["L0_attn_x"])}
    x = nc.dram_tensor("x", (B, S, D), F32, kind="ExternalInput").ap()
    y = nc.dram_tensor("y", (B, S, D), F32, kind="ExternalOutput").ap()
    stage_inputs = []
    for stage, laid in layouts(arrays).items():
        aps = {}
        for name, a in laid.items():
            fed[f"in_{stage}_{name}"] = np.ascontiguousarray(a)
            aps[name] = nc.dram_tensor(f"in_{stage}_{name}", a.shape, F32, kind="ExternalInput").ap()
        stage_inputs.append(aps)
    two_layers(nc, x, y, stage_inputs)
    result = run_bass_kernel_spmd(nc, [fed], core_ids=[0])
    return result.results[0]["y"]
```
